# Optimizing a Trainium2 kernel written in Bass

```python
import numpy as np
import jax
import jax.numpy as jnp

def _softmax(x, axis=-1):
    return jax.nn.softmax(x, axis=axis)
def _gelu(x):
    return jax.nn.gelu(x, approximate=True)
def _silu(x):
    return jax.nn.silu(x)
def _sigmoid(x):
    return jax.nn.sigmoid(x)
def _layernorm(x, axis=-1, eps=1e-5):
    m = jnp.mean(x, axis=axis, keepdims=True)
    v = jnp.var(x, axis=axis, keepdims=True)
    return (x - m) / jnp.sqrt(v + eps)
def _scatter_add(tgt, idx, src, axis=0):
    return tgt.at[idx].add(src)
def _segment_sum(src, seg, n):
    return jax.ops.segment_sum(src, seg, n)

kernel_name = 'mk_conv_preact_d2_conv_nchw128_c65457'

def setup_inputs(seed: int = 0):
    np.random.seed(seed)
    _w = jnp.asarray
    def _rec_inputs():
        import jax
        import jax.numpy as jnp
        _gk = jax.random.key(seed)
        x = 7.22e-05 + 1 * jax.random.normal(jax.random.fold_in(_gk, 1), (4, 128, 128, 128), jnp.float32)
        return x
    x = _rec_inputs()
    def _L0_conv_setup():
        import jax, jax.numpy as jnp
        import numpy as np
        DIM, D_STATE, D_CONV, EXPAND = (128, 16, 4, 2)
        D_INNER = EXPAND * DIM
        DT_RANK = (DIM + 15) // 16

        def _mamba(xn, W_in, conv_w, conv_b, W_xproj, W_dt, b_dt, A_log, D, W_out):
            Bsz, L, _ = xn.shape
            d_inner, d_conv = conv_w.shape
            d_state = A_log.shape[1]
            dt_rank = W_dt.shape[1]
            xz = xn @ W_in.T
            xin, z = jnp.split(xz, 2, axis=-1)
            xc = jnp.swapaxes(xin, 1, 2)
            xc = jax.lax.conv_general_dilated(xc, conv_w[:, None, :], window_strides=(1,), padding=[(d_conv - 1, 0)], feature_group_count=d_inner)
            xc = xc + conv_b[None, :, None]
            u = jax.nn.silu(jnp.swapaxes(xc, 1, 2))
            x_dbl = u @ W_xproj.T
            dt, Bm, Cm = jnp.split(x_dbl, [dt_rank, dt_rank + d_state], axis=-1)
            delta = jax.nn.softplus(dt @ W_dt.T + b_dt)
            A = -jnp.exp(A_log)

            def step(h, xs):
                d_t, B_t, C_t, u_t = xs
                dA = jnp.exp(d_t[..., None] * A)
                h = dA * h + (d_t * u_t)[..., None] * B_t[:, None, :]
                y = jnp.einsum('bdn,bn->bd', h, C_t)
                return (h, y)
            xs = (jnp.swapaxes(delta, 0, 1), jnp.swapaxes(Bm, 0, 1), jnp.swapaxes(Cm, 0, 1), jnp.swapaxes(u, 0, 1))
            h0 = jnp.zeros((Bsz, d_inner, d_state), delta.dtype)
            _, ys = jax.lax.scan(step, h0, xs)
            y = jnp.swapaxes(ys, 0, 1) + u * D
            y = y * jax.nn.silu(z)
            return y @ W_out.T
        key = jax.random.key(seed)
        ks = jax.random.split(key, 8)
        B, H, W = (4, 128, 128)
        x = jax.random.normal(ks[0], (B, DIM, H, W), dtype=jnp.float32)
        W_in = jax.random.normal(ks[1], (2 * D_INNER, DIM)) / np.sqrt(DIM)
        conv_w = jax.random.normal(ks[2], (D_INNER, D_CONV)) / np.sqrt(D_CONV)
        conv_b = jnp.zeros((D_INNER,), jnp.float32)
        W_xproj = jax.random.normal(ks[3], (DT_RANK + 2 * D_STATE, D_INNER)) / np.sqrt(D_INNER)
        W_dt = jax.random.normal(ks[4], (D_INNER, DT_RANK)) / np.sqrt(DT_RANK)
        b_dt = jax.random.normal(ks[5], (D_INNER,)) * 0.1
        A_log = jnp.log(jnp.tile(jnp.arange(1, D_STATE + 1, dtype=jnp.float32), (D_INNER, 1)))
        Dskip = jnp.ones((D_INNER,), jnp.float32)
        W_out = jax.random.normal(ks[6], (DIM, D_INNER)) / np.sqrt(D_INNER)
        return {'x': x, 'ln_w': jnp.ones((DIM,), jnp.float32), 'ln_b': jnp.zeros((DIM,), jnp.float32), 'W_in': W_in, 'conv_w': conv_w, 'conv_b': conv_b, 'W_xproj': W_xproj, 'W_dt': W_dt, 'b_dt': b_dt, 'A_log': A_log, 'D': Dskip, 'W_out': W_out}
    _L0_conv_all = _L0_conv_setup()
    _L0_conv_in = {k: v for k, v in _L0_conv_all.items() if k in ('ln_w', 'ln_b', 'W_in', 'conv_w', 'conv_b', 'W_xproj', 'W_dt', 'b_dt', 'A_log', 'D', 'W_out', )}
    del _L0_conv_all

    def _L1_conv_setup():
        import jax, jax.numpy as jnp
        import numpy as np
        LRELU_SLOPE = 0.01

        def _lrelu(x):
            return jnp.where(x >= 0, x, LRELU_SLOPE * x)

        def _conv1x1(x, w, b):
            return jnp.einsum('oc,bc...->bo...', w, x) + b.reshape((1, -1) + (1,) * (x.ndim - 2))
        key = jax.random.key(seed)
        ks = jax.random.split(key, 16)

        def p(k, shape, fan_in):
            bound = 1.0 / np.sqrt(fan_in)
            return jax.random.uniform(k, shape, jnp.float32, -bound, bound)
        x = jax.random.normal(ks[0], (4, 128, 128, 128), jnp.float32)
        return {'x': x, 'sw1': p(ks[1], (64, 128), 128), 'sb1': p(ks[2], (64,), 128), 'sw2': p(ks[3], (32, 64), 64), 'sb2': p(ks[4], (32,), 64), 'sw3': p(ks[5], (16, 32), 32), 'sb3': p(ks[6], (16,), 32), 'mw1': p(ks[7], (32, 17), 17), 'mb1': p(ks[8], (32,), 17), 'mw2': p(ks[9], (32, 32), 32), 'mb2': p(ks[10], (32,), 32), 'mw3': p(ks[11], (16, 32), 32), 'mb3': p(ks[12], (16,), 32), 'mw4': p(ks[13], (1, 16), 16), 'mb4': p(ks[14], (1,), 16)}
    _L1_conv_all = _L1_conv_setup()
    _L1_conv_in = {k: v for k, v in _L1_conv_all.items() if k in ('sw1', 'sb1', 'sw2', 'sb2', 'sw3', 'sb3', 'mw1', 'mb1', 'mw2', 'mb2', 'mw3', 'mb3', 'mw4', 'mb4', )}
    del _L1_conv_all

    return {
        "x": x,
        "L0_conv_ln_w": _L0_conv_in["ln_w"],
        "L0_conv_ln_b": _L0_conv_in["ln_b"],
        "L0_conv_W_in": _L0_conv_in["W_in"],
        "L0_conv_conv_w": _L0_conv_in["conv_w"],
        "L0_conv_conv_b": _L0_conv_in["conv_b"],
        "L0_conv_W_xproj": _L0_conv_in["W_xproj"],
        "L0_conv_W_dt": _L0_conv_in["W_dt"],
        "L0_conv_b_dt": _L0_conv_in["b_dt"],
        "L0_conv_A_log": _L0_conv_in["A_log"],
        "L0_conv_D": _L0_conv_in["D"],
        "L0_conv_W_out": _L0_conv_in["W_out"],
        "L1_conv_sw1": _L1_conv_in["sw1"],
        "L1_conv_sb1": _L1_conv_in["sb1"],
        "L1_conv_sw2": _L1_conv_in["sw2"],
        "L1_conv_sb2": _L1_conv_in["sb2"],
        "L1_conv_sw3": _L1_conv_in["sw3"],
        "L1_conv_sb3": _L1_conv_in["sb3"],
        "L1_conv_mw1": _L1_conv_in["mw1"],
        "L1_conv_mb1": _L1_conv_in["mb1"],
        "L1_conv_mw2": _L1_conv_in["mw2"],
        "L1_conv_mb2": _L1_conv_in["mb2"],
        "L1_conv_mw3": _L1_conv_in["mw3"],
        "L1_conv_mb3": _L1_conv_in["mb3"],
        "L1_conv_mw4": _L1_conv_in["mw4"],
        "L1_conv_mb4": _L1_conv_in["mb4"],
    }

def reference(x, L0_conv_ln_w, L0_conv_ln_b, L0_conv_W_in, L0_conv_conv_w, L0_conv_conv_b, L0_conv_W_xproj, L0_conv_W_dt, L0_conv_b_dt, L0_conv_A_log, L0_conv_D, L0_conv_W_out, L1_conv_sw1, L1_conv_sb1, L1_conv_sw2, L1_conv_sb2, L1_conv_sw3, L1_conv_sb3, L1_conv_mw1, L1_conv_mb1, L1_conv_mw2, L1_conv_mb2, L1_conv_mw3, L1_conv_mb3, L1_conv_mw4, L1_conv_mb4):
    import jax
    import jax.numpy as jnp
    def _L0_conv_ref(x, ln_w, ln_b, W_in, conv_w, conv_b, W_xproj, W_dt, b_dt, A_log, D, W_out):
        import jax, jax.numpy as jnp
        import numpy as np
        DIM, D_STATE, D_CONV, EXPAND = (128, 16, 4, 2)
        D_INNER = EXPAND * DIM
        DT_RANK = (DIM + 15) // 16

        def _mamba(xn, W_in, conv_w, conv_b, W_xproj, W_dt, b_dt, A_log, D, W_out):
            Bsz, L, _ = xn.shape
            d_inner, d_conv = conv_w.shape
            d_state = A_log.shape[1]
            dt_rank = W_dt.shape[1]
            xz = xn @ W_in.T
            xin, z = jnp.split(xz, 2, axis=-1)
            xc = jnp.swapaxes(xin, 1, 2)
            xc = jax.lax.conv_general_dilated(xc, conv_w[:, None, :], window_strides=(1,), padding=[(d_conv - 1, 0)], feature_group_count=d_inner)
            xc = xc + conv_b[None, :, None]
            u = jax.nn.silu(jnp.swapaxes(xc, 1, 2))
            x_dbl = u @ W_xproj.T
            dt, Bm, Cm = jnp.split(x_dbl, [dt_rank, dt_rank + d_state], axis=-1)
            delta = jax.nn.softplus(dt @ W_dt.T + b_dt)
            A = -jnp.exp(A_log)

            def step(h, xs):
                d_t, B_t, C_t, u_t = xs
                dA = jnp.exp(d_t[..., None] * A)
                h = dA * h + (d_t * u_t)[..., None] * B_t[:, None, :]
                y = jnp.einsum('bdn,bn->bd', h, C_t)
                return (h, y)
            xs = (jnp.swapaxes(delta, 0, 1), jnp.swapaxes(Bm, 0, 1), jnp.swapaxes(Cm, 0, 1), jnp.swapaxes(u, 0, 1))
            h0 = jnp.zeros((Bsz, d_inner, d_state), delta.dtype)
            _, ys = jax.lax.scan(step, h0, xs)
            y = jnp.swapaxes(ys, 0, 1) + u * D
            y = y * jax.nn.silu(z)
            return y @ W_out.T
        Bsz, d_model = x.shape[:2]
        img_dims = x.shape[2:]
        L = int(np.prod(img_dims))
        xf = jnp.swapaxes(x.reshape(Bsz, d_model, L), 1, 2)
        mu = jnp.mean(xf, axis=-1, keepdims=True)
        var = jnp.mean(jnp.square(xf - mu), axis=-1, keepdims=True)
        xn = (xf - mu) * jax.lax.rsqrt(var + 1e-05) * ln_w + ln_b
        y = _mamba(xn, W_in, conv_w, conv_b, W_xproj, W_dt, b_dt, A_log, D, W_out)
        return jnp.swapaxes(y, 1, 2).reshape(x.shape)

    def _L1_conv_ref(x, sw1, sb1, sw2, sb2, sw3, sb3, mw1, mb1, mw2, mb2, mw3, mb3, mw4, mb4):
        import jax, jax.numpy as jnp
        import numpy as np
        LRELU_SLOPE = 0.01

        def _lrelu(x):
            return jnp.where(x >= 0, x, LRELU_SLOPE * x)

        def _conv1x1(x, w, b):
            return jnp.einsum('oc,bc...->bo...', w, x) + b.reshape((1, -1) + (1,) * (x.ndim - 2))
        B = x.shape[0]
        D = 128
        f = _lrelu(_conv1x1(x, sw1, sb1))
        f = _lrelu(_conv1x1(f, sw2, sb2))
        f = _conv1x1(f, sw3, sb3)
        pts = jnp.linspace(-1.0, 1.0, D, dtype=f.dtype).reshape(1, 1, D, 1, 1)
        pts = jnp.broadcast_to(pts, (B, 1, D, D, D))
        feat = jnp.broadcast_to(f[:, :, None, :, :], (B, 16, D, D, D))
        feat = jnp.concatenate([feat, pts], axis=1).reshape(B, 17, -1)
        h = _lrelu(_conv1x1(feat, mw1, mb1))
        h = _lrelu(_conv1x1(h, mw2, mb2))
        h = _lrelu(_conv1x1(h, mw3, mb3))
        sdf = jax.nn.sigmoid(_conv1x1(h, mw4, mb4))
        return sdf.reshape(B, D, D, D)

    def _gn(v, G=32, eps=1e-5):
        B_, C_, H_, W_ = v.shape
        g = v.reshape(B_, G, C_ // G, H_, W_)
        m = jnp.mean(g, axis=(2, 3, 4), keepdims=True)
        s = jnp.var(g, axis=(2, 3, 4), keepdims=True)
        return ((g - m) / jnp.sqrt(s + eps)).reshape(v.shape)

    def _ln_c(v, eps=1e-6):
        m = jnp.mean(v, axis=1, keepdims=True)
        s = jnp.var(v, axis=1, keepdims=True)
        return (v - m) / jnp.sqrt(s + eps)

    def _ln_t(v, eps=1e-5):
        m = jnp.mean(v, axis=-1, keepdims=True)
        s = jnp.var(v, axis=-1, keepdims=True)
        return (v - m) / jnp.sqrt(s + eps)

    def _to_tokens(v):
        B_, C_, H_, W_ = v.shape
        return v.reshape(B_, C_, H_ * W_).transpose(0, 2, 1)
    def _from_tokens(t, like):
        B_, C_, H_, W_ = like.shape
        return t.transpose(0, 2, 1).reshape(B_, C_, H_, W_)

    x = x + _L0_conv_ref(_gn(x), L0_conv_ln_w, L0_conv_ln_b, L0_conv_W_in, L0_conv_conv_w, L0_conv_conv_b, L0_conv_W_xproj, L0_conv_W_dt, L0_conv_b_dt, L0_conv_A_log, L0_conv_D, L0_conv_W_out)
    x = x + _L1_conv_ref(_gn(x), L1_conv_sw1, L1_conv_sb1, L1_conv_sw2, L1_conv_sb2, L1_conv_sw3, L1_conv_sb3, L1_conv_mw1, L1_conv_mb1, L1_conv_mw2, L1_conv_mb2, L1_conv_mw3, L1_conv_mb3, L1_conv_mw4, L1_conv_mb4)
    return x


_drawn_inputs = setup_inputs


def setup_inputs(seed=0):
    import zlib

    import numpy as np

    out = dict(_drawn_inputs(seed))
    spreads = {'L0_conv_ln_w': (1.0, 0.2),
     'L0_conv_ln_b': (0.0, 0.1),
     'L0_conv_conv_b': (0.0, 0.1),
     'L0_conv_D': (1.0, 0.2)}
    factors = {'L1_conv_sw1': 8.0,
     'L1_conv_sb1': 8.0,
     'L1_conv_sw2': 8.0,
     'L1_conv_sb2': 34.422,
     'L1_conv_sw3': 8.0,
     'L1_conv_sb3': 59.31,
     'L1_conv_mw1': 8.0,
     'L1_conv_mb1': 176.254,
     'L1_conv_mw2': 8.0,
     'L1_conv_mb2': 200.0,
     'L1_conv_mw3': 8.0,
     'L1_conv_mb3': 200.0,
     'L1_conv_mw4': 8.0}
    for name, (base, spread) in spreads.items():
        noise = np.random.default_rng([zlib.crc32(name.encode()), seed]).standard_normal(out[name].shape)
        drawn = base * np.exp(spread * noise) if base else spread * noise
        out[name] = jnp.asarray(drawn.astype(out[name].dtype))
    for name, factor in factors.items():
        out[name] = (out[name] * factor).astype(out[name].dtype)
    return out
```

```python
from contextlib import ExitStack

import concourse.bass as bass
from concourse import mybir

F32 = mybir.dt.float32
BF16 = mybir.dt.bfloat16
ALU = mybir.AluOpType
ACT = mybir.ActivationFunctionType

P = 128
L = 512
NS = 16
TAPS = 4
DTR = 8
LAG = 2
GQ = 4
NG = 8
SLOPE = 0.01
SOFTPLUS_LINEAR = 20.0
SIGMOID_ZERO = -44.0
EPS = 1e-5


def mamba_sdf_kernel(nc, x, w_in_t, conv_w_t, conv_b, ln_w, ln_b, w_xproj_t, w_dt_t, b_dt, a_log,
                     d_skip, w_out_t, sw1_t, sb1, sw2_t, sb2, sw3, sb3, mw1_t, mw1_pt, mb1, mw2_bd, mb2,
                     mw3_bd, mb3, mw4_bd, mb4, center, group_mean, ones_mean, ident, pick, points, out):
    B, _, N = x.shape
    T = N // L
    PAIRS = T // 2

    with ExitStack() as ctx:
        def sb(name, shape, dt=F32):
            return ctx.enter_context(nc.sbuf_tensor(name, shape, dt))

        def sem(name):
            return ctx.enter_context(nc.semaphore(name))

        w_z = sb("w_z", [P, 2 * P])
        w_conv = sb("w_conv", [P, TAPS, 2, P])
        cb = sb("cb", [P, 2])
        lnw = sb("lnw", [P, 1])
        lnb = sb("lnb", [P, 1])
        w_xp = sb("w_xp", [P, 2, 104])
        w_dt = sb("w_dt", [104, 2, P])
        bdt = sb("bdt", [P, 2])
        a_neg = sb("a_neg", [P, 2, NS])
        dsk = sb("dsk", [P, 2])
        w_out = sb("w_out", [P, 2, P])
        cen = sb("cen", [P, P])
        gmean = sb("gmean", [P, P])
        omean = sb("omean", [P, P])
        idn = sb("idn", [P, P])
        pk = sb("pk", [96, 2 * NS, P], BF16)
        s1 = sb("s1", [P, 64])
        bs1 = sb("bs1", [64, 1])
        s2 = sb("s2", [64, 32])
        bs2 = sb("bs2", [32, 1])
        s3 = sb("s3", [16, 32])
        bs3 = sb("bs3", [16, 1])
        m1 = sb("m1", [16, P])
        m1p = sb("m1p", [P, 1])
        bm1 = sb("bm1", [P, 1])
        m2 = sb("m2", [P, P])
        bm2 = sb("bm2", [P, 1])
        m3 = sb("m3", [P, 64])
        bm3 = sb("bm3", [P, 1])
        m4 = sb("m4", [P, 4, 32])
        bm4 = sb("bm4", [P, 1])
        pts = sb("pts", [P, NG * GQ])
        ptb = sb("ptb", [P, NG * GQ])
        gw = sb("gw", [32, P])
        gb = sb("gb", [P, 1])
        epsc = sb("epsc", [P, 1])

        X = sb("X", [P, N])
        stats = sb("stats", [P, T, 6])
        mv = sb("mv", [P, 2])
        dev = sb("dev", [P, 1])
        vd = sb("vd", [P, 1])
        lnv = sb("lnv", [P, 1])
        gr = sb("gr", [P, 1])
        gs = sb("gs", [P, 1])
        cen_r = sb("cen_r", [P, P])
        cs = sb("cs", [P, 1])
        s1r = sb("s1r", [P, 64])
        b1r = sb("b1r", [64, 1])

        H = sb("H", [P, NS, 2, L])
        u = [sb(f"u{i}", [P, 2, L]) for i in range(2)]
        sz = [sb(f"sz{i}", [P, 2, L]) for i in range(2)]
        delta = sb("delta", [P, 2, L])
        du = sb("du", [P, 2, L])
        bc = [sb(f"bc{i}", [96, L], BF16) for i in range(2)]
        ln = sb("ln", [P, L])
        xnf = sb("xnf", [P, TAPS - 1 + L])
        ex = sb("ex", [P, 2, L])
        mid = ex[64:96, 0, 0:L // 2].bitcast(BF16)
        dts = sb("dts", [104, L])
        dbu = [sb(f"dbu{i}", [P, 2, L]) for i in range(2)]
        csb = [sb(f"csb{i}", [P, L]) for i in range(2)]
        ch = [sb(f"ch{i}", [P, 2, L]) for i in range(2)]
        w_x = csb[0][:, 0:2 * P]
        tapw = ch[0][:, :, :].rearrange("p h (k n) -> p (h k) n", n=2 * P)

        Hf = H[:, :, :, :].rearrange("p n h l -> p (n h l)")

        def over(k, n):
            return Hf[:, k * L:(k + n) * L]

        t1 = [over(4 * i, 4).rearrange("p (k l) -> p k l", k=GQ) for i in range(2)]
        t2 = [over(8 + 4 * i, 4).rearrange("p (k l) -> p k l", k=GQ) for i in range(2)]
        t3 = [over(16 + 2 * i, 2).rearrange("p (k l) -> p k l", k=2) for i in range(4)]
        g = [over(24 + i, 1) for i in range(2)]
        f1 = over(26, 1)[0:64]
        f2 = over(27, 1)[0:32]
        sg = over(28, 1)
        ob = [over(30 + i, 1) for i in range(2)]

        ps = ctx.enter_context(nc.psum_tensor("ps", [P, 8, L], F32))
        y_ps, pp, dA = ps[:, 0:2, :], ps[:, 2:4, :], ps[:, 4:6, :]
        B_ps, C_ps = ps[:, 6, :], ps[:, 7, :]
        m2_ps = [ps[:, 0:2, :], ps[:, 4:6, :]]
        m3_ps = ps[:, 6:8, :]
        m4_ps, f_ps = ps[:, 2, :], ps[:, 3, :]

        s_w = sem("s_weights_loaded")
        s_act0, s_dve0, s_pe0 = sem("s_act_setup"), sem("s_dve_setup"), sem("s_pe_setup")
        s_x = sem("s_x_loaded")
        s_carry = sem("s_carry_wait")
        s_mv, s_gm, s_vd, s_gv = sem("s_mean_var"), sem("s_group_mean"), sem("s_group_dev"), sem("s_group_var")
        s_dev, s_lnv, s_gr, s_gs = sem("s_dev"), sem("s_log_var"), sem("s_group_rstd"), sem("s_group_shift")
        s_nw, s_cs, s_nb = sem("s_norm_weights"), sem("s_shift_product"), sem("s_norm_bias")
        s_st, s_agg, s_h0 = sem("s_stats"), sem("s_aggregated"), sem("s_state_cleared")
        s_cen, s_sq, s_var, s_lv, s_rs = sem("s_centered"), sem("s_squared"), sem("s_variance"), sem("s_logvar"), sem("s_rstd")
        s_xn, s_car, s_xnf = sem("s_normed"), sem("s_carried"), sem("s_affine")
        s_z, s_kz, s_ez, s_lz, s_rz, s_sz = sem("s_z"), sem("s_limited_z"), sem("s_exp_z"), sem("s_log_z"), sem("s_sigmoid_z"), sem("s_silu_z")
        s_cv, s_kc, s_ec, s_lc, s_rc, s_u = sem("s_conv"), sem("s_limited_c"), sem("s_exp_c"), sem("s_log_c"), sem("s_sigmoid_c"), sem("s_u")
        s_xd, s_hi, s_dts, s_rest, s_mid, s_lo = sem("s_xdbl"), sem("s_bc_high"), sem("s_dt_copied"), sem("s_bc_rest"), sem("s_bc_mid"), sem("s_bc_low")
        s_dt, s_tm, s_ed, s_sp, s_del, s_du = sem("s_dt"), sem("s_clamped"), sem("s_exp_dt"), sem("s_log_dt"), sem("s_delta"), sem("s_delta_u")
        s_B, s_C, s_mulb, s_dA0, s_dA1 = sem("s_B_spread"), sem("s_C_spread"), sem("s_dBu"), sem("s_decay0"), sem("s_decay1")
        s_dA = [s_dA0, s_dA1]
        s_scan = [sem("s_scan0"), sem("s_scan1")]
        s_Ccp, s_ch, s_sum = sem("s_C_copied"), sem("s_Ch"), sem("s_summed")
        s_yv, s_gate, s_o, s_res, s_st1 = sem("s_y_out"), sem("s_gated"), sem("s_projected"), sem("s_residual"), sem("s_stats1")
        s_f1, s_f1a, s_f1l = sem("s_f1"), sem("s_f1_biased"), sem("s_f1_relu")
        s_f2, s_f2a, s_f2l = sem("s_f2"), sem("s_f2_biased"), sem("s_f2_relu")
        s_gp, s_g = sem("s_g_product"), sem("s_g")
        s_t1, s_l1, s_m2 = sem("s_h1_biased"), sem("s_h1"), sem("s_mm2")
        s_t2, s_l2, s_m3 = sem("s_h2_biased"), sem("s_h2"), sem("s_mm3")
        s_t3, s_l3, s_m4 = sem("s_h3_biased"), sem("s_h3"), sem("s_mm4")
        s_lim = sem("s_sdf_limited")
        s_e, s_le, s_sg, s_ob, s_out = sem("s_sdf_exp"), sem("s_sdf_log"), sem("s_sdf"), sem("s_out_ready"), [sem("s_out_stored0"), sem("s_out_stored1")]

        pe_counts = {s_cen: 1, s_var: 1, s_z: 1, s_cv: 2, s_xd: 1, s_dt: 1, s_B: NS, s_C: NS, s_sum: NS, s_o: 1,
                     s_f1: 1, s_f2: 1, s_gp: 1, s_m2: 2 * NG, s_m3: NG, s_m4: NG // 2}
        act_counts = {s_sq: 1, s_lv: 1, s_rs: 1, s_ez: 1, s_lz: 1, s_rz: 1, s_ec: 1, s_lc: 1, s_rc: 1, s_hi: 1, s_dts: 1,
                      s_ed: 1, s_sp: 1, s_dA0: NS, s_dA1: NS, s_Ccp: NS, s_f1a: 1, s_f2a: 1, s_g: 1,
                      s_t1: NG, s_t2: 2 * NG, s_t3: NG, s_e: 1, s_le: 1, s_sg: 1}
        pool_counts = {s_ch: NS, s_gate: 1}
        dve_counts = {s_xn: 1, s_car: 1, s_xnf: 1, s_kz: 1, s_sz: 1, s_kc: 1, s_u: 1, s_rest: 1, s_mid: 2, s_lo: 1,
                      s_tm: 1, s_del: 1, s_du: 1, s_mulb: NS, s_scan[0]: NS, s_scan[1]: NS, s_yv: 1, s_res: 1, s_st1: 1,
                      s_f1l: 1, s_f2l: 1, s_l1: NG, s_l2: NG, s_l3: NG, s_lim: 1, s_ob: 1}

        def chunk_zero(eng, counts):
            for s, n in counts.items():
                eng.sem_inc(s, n)

        loads = [
            (w_x, w_in_t[:, 0:2 * P]), (w_z[:], w_in_t[:, 2 * P:4 * P]), (tapw, conv_w_t.partition_broadcast(P)), (cb[:], conv_b), (lnw[:], ln_w), (lnb[:], ln_b),
            (w_xp[:], w_xproj_t), (w_dt[96:104], w_dt_t), (bdt[:], b_dt), (a_neg[:], a_log), (dsk[:], d_skip),
            (w_out[:], w_out_t), (cen[:], center), (gmean[:], group_mean), (omean[:], ones_mean), (idn[:], ident),
            (pk[:], pick), (s1[:], sw1_t), (bs1[:], sb1), (s2[:], sw2_t), (bs2[:], sb2), (s3[:], sw3), (bs3[:], sb3),
            (m1[:], mw1_t), (m1p[:], mw1_pt), (bm1[:], mb1), (m2[:], mw2_bd), (bm2[:], mb2), (m3[:], mw3_bd),
            (bm3[:], mb3), (m4[:], mw4_bd), (bm4[:], mb4), (pts[:], points),
        ]
        W_ALL = 16 * len(loads)
        XPARTS = 8

        def fresh(eng, value):
            return eng.snap(eng.to_reg(value))

        def plain(eng):
            eng.sem_inc(s_carry, 1)

        def walk(eng, b, chunk):
            for par in range(2):
                chunk(fresh(eng, b * T + (1 + par)), fresh(eng, b * PAIRS + 1), par, par * L, par, par == 0, False)
            with eng.Fori(1, PAIRS - 1) as j:
                for par in range(2):
                    chunk(fresh(eng, b * T + j * 2 + (1 + par)), fresh(eng, b * PAIRS + j + 1), j * 2 + par,
                          fresh(eng, j * (2 * L) + par * L), par, False, False)
            for par in range(2):
                i = T - 2 + par
                chunk(fresh(eng, b * T + (i + 1)), fresh(eng, b * PAIRS + PAIRS), i, i * L, par, False, par == 1)

        block = ctx.enter_context(nc.Block())

        @block.sync
        def _(sp):
            chunk_zero(sp, {s_out[0]: 16, s_out[1]: 16})
            for dst, src in loads:
                sp.dma_start(dst, src).then_inc(s_w, 16)
            with sp.Fori(0, B) as b:
                sp.wait_ge(s_ob, b * T + 1)
                for k in range(XPARTS):
                    w = N // XPARTS
                    sp.dma_start(X[:, k * w:(k + 1) * w], x[b, :, k * w:(k + 1) * w]).then_inc(s_x, 16)

                def chunk(t, pair, i, col, par, first, last):
                    sp.wait_ge(s_ob, t + 1)
                    sp.dma_start(out[b, :, bass.ds(col, L)], ob[par]).then_inc(s_out[par], 16)

                walk(sp, b, chunk)
            for par in range(2):
                sp.wait_ge(s_out[par], 16 * (B * PAIRS + 1))

        @block.tensor
        def _(pe):
            mm = nc.tensor.matmul
            chunk_zero(pe, pe_counts)

            pe.wait_ge(s_w, W_ALL)
            mm(ps[0:32, 0, 0:P], s3[:, :], m1[:, :], start=True, stop=True).then_inc(s_pe0, 1)
            mm(ps[:, 1, 0:1], m1[:, :], bs3[:, :], start=True, stop=True).then_inc(s_pe0, 1)

            def group_norm(k, weights, width):
                pe.wait_ge(s_mv, k + 1)
                mm(pp[:, 0, 0:1], gmean[:, :], mv[:, 0:1], start=True, stop=True).then_inc(s_gm, 1)
                pe.wait_ge(s_vd, k + 1)
                mm(pp[:, 1, 0:1], gmean[:, :], vd[:, :], start=True, stop=True).then_inc(s_gv, 1)
                pe.wait_ge(s_gs, k + 1)
                mm(ps[0:width, 7, 0:1], weights, gs[:, :], start=True, stop=True).then_inc(s_cs, 1)

            def prep(t, col):
                def center_it():
                    pe.wait_ge(s_del, t)
                    pe.wait_ge(s_du, t)
                    mm(pp[:, 0, :], cen_r[:, :], X[:, bass.ds(col, L)], start=True, stop=True).then_inc(s_cen, 1)

                def variance():
                    pe.wait_ge(s_sq, t + 1)
                    mm(pp[:, 1, :], omean[:, :], ln[:, :], start=True, stop=True).then_inc(s_var, 1)

                def z():
                    pe.wait_ge(s_xnf, t + 1)
                    for h in range(2):
                        m = mm(pp[:, h, :], w_z[:, h * P:(h + 1) * P], xnf[:, TAPS - 1:], start=True, stop=True)
                    m.then_inc(s_z, 1)

                def conv(h, a):
                    if h == 0 and a == 0:
                        pe.wait_ge(s_sz, t + 1)
                    for k in range(a, a + 2):
                        m = mm(pp[:, h, :], w_conv[:, k, h, :], xnf[:, k:k + L], start=k == 0, stop=k == TAPS - 1)
                    if a == 2:
                        m.then_inc(s_cv, 1)

                def xdbl():
                    pe.wait_ge(s_u, t + 1)
                    for h in range(2):
                        m = mm(pp[0:104, 0, :], w_xp[:, h, :], u_of(t)[:, h, :], start=h == 0, stop=h == 1)
                    m.then_inc(s_xd, 1)

                def step_size():
                    pe.wait_ge(s_dts, t + 1)
                    pe.wait_ge(s_rest, t + 1)
                    for h in range(2):
                        m = mm(pp[:, h, :], w_dt[96:104, h, :], dts[96:104, :], start=True, stop=True)
                    m.then_inc(s_dt, 1)

                return center_it, variance, z, conv, xdbl, step_size

            par_now = [0]

            def u_of(t):
                return u[par_now[0]]

            def spread(t, n, par):
                if n == 0:
                    pe.wait_ge(s_lo, t + 1)
                pe.wait_ge(s_mulb, t * NS + n)
                mm(B_ps, pk[:, n, :], bc[par][:, :], start=True, stop=True).then_inc(s_B, 1)
                pe.wait_ge(s_Ccp, t * NS + n)
                mm(C_ps, pk[:, NS + n, :], bc[par][:, :], start=True, stop=True).then_inc(s_C, 1)

            def add_state(t, n):
                if n == 0:
                    pe.wait_ge(s_yv, t)
                pe.wait_ge(s_ch, t * NS + (n + 1))
                for h in range(2):
                    m = mm(y_ps[:, h, :], idn[:, :], ch[n % 2][:, h, :], start=n == 0, stop=n == NS - 1)
                m.then_inc(s_sum, 1)

            def project_out(t):
                pe.wait_ge(s_gate, t + 1)
                for h in range(2):
                    m = mm(pp[:, 1, :], w_out[:, h, :], ex[:, h, :], start=h == 0, stop=h == 1)
                m.then_inc(s_o, 1)

            def layer0(t, pair, i, col, par, first, last):
                par_now[0] = 1 - par
                if not last:
                    cen_, var_, z_, conv_, xd_, dt_ = prep(t + 1, col + L)
                for n in range(NS):
                    spread(t, n, par)
                    if n == 0 and not last:
                        cen_()
                    if n == 1 and not last:
                        var_()
                    if n >= LAG:
                        add_state(t, n - LAG)
                    elif not first:
                        add_state(t - 1, NS - LAG + n)
                    if n == 3 and not first:
                        if not last:
                            pe.wait_ge(s_lv, t + 2)
                        project_out(t - 1)
                    if not last:
                        if n == 5:
                            if not first:
                                pe.wait_ge(s_res, t)
                            z_()
                        if n == 8:
                            conv_(0, 0)
                            conv_(0, 2)
                        if n in (9, 10):
                            conv_(1, 2 * (n - 9))
                        if n == 12:
                            xd_()
                        if n == 13:
                            dt_()

            def layer0_start(t):
                par_now[0] = 0
                cen_, var_, z_, conv_, xd_, dt_ = prep(t, 0)
                cen_()
                var_()
                z_()
                for h in range(2):
                    for a in (0, 2):
                        conv_(h, a)
                xd_()
                dt_()

            def layer0_end(t):
                for n in range(NS - LAG, NS):
                    add_state(t, n)
                project_out(t)

            def features(t, col, par):
                def first_layer():
                    pe.wait_ge(s_g, t)
                    mm(f_ps[0:64], s1r[:, :], X[:, bass.ds(col, L)], start=True, stop=True).then_inc(s_f1, 1)

                def second_layer():
                    pe.wait_ge(s_f1l, t + 1)
                    plain(pe)
                    mm(f_ps[0:32], s2[:, :], f1, start=True, stop=True).then_inc(s_f2, 1)

                def third_layer():
                    pe.wait_ge(s_f2l, t + 1)
                    mm(f_ps, gw[:, :], f2, start=True, stop=True).then_inc(s_gp, 1)

                return first_layer, second_layer, third_layer

            def mm2(t, k):
                pe.wait_ge(s_l1, t * NG + (k + 1))
                for half in range(2):
                    pe.wait_ge(s_t2, t * (2 * NG) + (2 * k + half))
                    for j in range(2):
                        q = 2 * half + j
                        m = mm(m2_ps[half][:, j, :], m2[:, :], t1[k % 2][:, q, :], start=True, stop=True)
                    m.then_inc(s_m2, 1)

            def mm3(t, k):
                pe.wait_ge(s_l2, t * NG + (k + 1))
                pe.wait_ge(s_t3, t * NG + k)
                for s in range(2):
                    for e in range(2):
                        m = mm(m3_ps[64 * e:64 * e + 64, s, :], m3[:, :], t2[k % 2][:, 2 * s + e, :],
                               start=True, stop=True)
                m.then_inc(s_m3, 1)

            def mm4(t, k):
                pe.wait_ge(s_l3, t * NG + (k + 1))
                if k == 1:
                    pe.wait_ge(s_lim, t)
                for quadrant in range(4):
                    m = mm(m4_ps[32 * quadrant:32 * quadrant + 32, :], m4[:, k // 2, :],
                           t3[(k - 1 + quadrant // 2) % 4][:, quadrant % 2, :], start=k == 1, stop=k == NG - 1)
                m.then_inc(s_m4, 1)

            def layer1(t, pair, i, col, par, first, last):
                f_a, f_b, f_c = features(t + 1, col + L, 1 - par)
                for k in range(NG):
                    mm2(t, k)
                    if k >= 1:
                        mm3(t, k - 1)
                    elif not first:
                        mm3(t - 1, NG - 1)
                    if k % 2 == 1 and k >= 3:
                        mm4(t, k - 2)
                    if k == 1 and not first:
                        mm4(t - 1, NG - 1)
                    if not last:
                        if k == 2:
                            f_a()
                        if k == 4:
                            f_b()
                        if k == 6:
                            f_c()

            with pe.Fori(0, B) as b:
                t0 = fresh(pe, b * T + 1)
                pe.wait_ge(s_w, W_ALL)
                group_norm(b * 2, cen[:, :], P)
                pe.wait_ge(s_nb, b * 2 + 1)
                layer0_start(t0)
                walk(pe, b, layer0)
                layer0_end(fresh(pe, b * T + T))
                group_norm(b * 2 + 1, s1[:, :], 64)
                pe.wait_ge(s_nb, b * 2 + 2)
                plain(pe)
                for f in features(fresh(pe, b * T + 1), 0, 0):
                    f()
                walk(pe, b, layer1)
                t9 = fresh(pe, b * T + T)
                mm3(t9, NG - 1)
                mm4(t9, NG - 1)

        @block.scalar
        def _(act):
            A = nc.scalar.activation
            chunk_zero(act, act_counts)
            nc.scalar.preload_act_table_set("natural_log_exp_and_others")
            act.wait_ge(s_w, W_ALL)
            A(a_neg[:, :, :], a_neg[:, :, :], ACT.Exp).then_inc(s_act0, 1)

            def group_norm(k):
                act.wait_ge(s_gv, k + 1)
                A(lnv[:, :], pp[:, 1, 0:1], ACT.Ln, bias=epsc[:, :]).then_inc(s_lnv, 1)
                act.wait_ge(s_lnv, k + 1)
                A(gr[:, :], lnv[:, :], ACT.Exp, scale=-0.5).then_inc(s_gr, 1)

            def prep(t):
                def square():
                    act.wait_ge(s_cen, t + 1)
                    act.wait_ge(s_lo, t)
                    A(ln[:, :], pp[:, 0, :], ACT.Square, bias=cs[:, :]).then_inc(s_sq, 1)

                def rstd():
                    act.wait_ge(s_var, t + 1)
                    A(ln[:, :], pp[:, 1, :], ACT.Ln, bias=epsc[:, :]).then_inc(s_lv, 1)
                    act.wait_ge(s_lv, t + 1)
                    A(ln[:, :], ln[:, :], ACT.Exp, scale=-0.5).then_inc(s_rs, 1)

                def sigmoid(limited, exp, log, done):
                    act.wait_ge(limited, t + 1)
                    A(ex[:, :, :], ex[:, :, :], ACT.Exp, scale=-1.0).then_inc(exp, 1)
                    act.wait_ge(exp, t + 1)
                    A(ex[:, :, :], ex[:, :, :], ACT.Ln, bias=1.0).then_inc(log, 1)
                    act.wait_ge(log, t + 1)
                    A(ex[:, :, :], ex[:, :, :], ACT.Exp, scale=-1.0).then_inc(done, 1)

                def sigmoid_z():
                    sigmoid(s_kz, s_ez, s_lz, s_rz)

                def sigmoid_c():
                    sigmoid(s_kc, s_ec, s_lc, s_rc)

                def parts(par):
                    act.wait_ge(s_xd, t + 1)
                    A(bc[par][:, :], pp[0:96, 0, :], ACT.Copy).then_inc(s_hi, 1)
                    act.wait_ge(s_dt, t)
                    A(dts[96:104, :], pp[96:104, 0, :], ACT.Copy).then_inc(s_dts, 1)

                def softplus():
                    act.wait_ge(s_tm, t + 1)
                    A(ex[:, :, :], ex[:, :, :], ACT.Exp).then_inc(s_ed, 1)
                    act.wait_ge(s_ed, t + 1)
                    A(ex[:, :, :], ex[:, :, :], ACT.Ln, bias=1.0).then_inc(s_sp, 1)

                return square, rstd, sigmoid_z, sigmoid_c, parts, softplus

            def layer0(t, pair, i, col, par, first, last):
                sq_, rs_, ez_, ec_, parts_, sp_ = prep(t + 1)
                act.wait_ge(s_del, t + 1)
                for n in range(NS):
                    for h in range(2):
                        act.wait_ge(s_scan[h], t * NS + n)
                        A(dA[:, h, :], delta[:, h, :], ACT.Exp, scale=a_neg[:, h, n:n + 1]).then_inc(s_dA[h], 1)
                    act.wait_ge(s_C, t * NS + (n + 1))
                    act.wait_ge(s_ch, t * NS + (n - 1))
                    A(csb[n % 2][:, :], C_ps, ACT.Copy).then_inc(s_Ccp, 1)
                    if not last:
                        if n == 0:
                            sq_()
                        if n == 2:
                            rs_()
                        if n == 6:
                            ez_()
                        if n == 11:
                            ec_()
                        if n == 12:
                            parts_(1 - par)
                        if n == 14:
                            sp_()

            def features(t, par):
                def first_layer():
                    act.wait_ge(s_f1, t + 1)
                    act.wait_ge(s_f2, t)
                    A(f1, f_ps[0:64], ACT.Identity, bias=b1r[:, :]).then_inc(s_f1a, 1)

                def second_layer():
                    act.wait_ge(s_f2, t + 1)
                    act.wait_ge(s_gp, t)
                    A(f2, f_ps[0:32], ACT.Identity, bias=bs2[:, :]).then_inc(s_f2a, 1)

                def third_layer():
                    act.wait_ge(s_gp, t + 1)
                    A(g[par], f_ps, ACT.Copy).then_inc(s_g, 1)

                return first_layer, second_layer, third_layer

            def bias1(t, k, par):
                if k == 0:
                    act.wait_ge(s_g, t + 1)
                act.wait_ge(s_m2, t * (2 * NG) + 2 * (k - 1))
                for q in range(GQ):
                    m = A(t1[k % 2][:, q, :], g[par], ACT.Identity, bias=ptb[:, GQ * k + q:GQ * k + q + 1])
                m.then_inc(s_t1, 1)

            def bias2(t, k):
                for half in range(2):
                    act.wait_ge(s_m2, t * (2 * NG) + (2 * k + half + 1))
                    if half == 0:
                        act.wait_ge(s_m3, t * NG + (k - 1))
                    A(t2[k % 2][:, 2 * half:2 * half + 2, :], m2_ps[half], ACT.Identity, bias=bm2[:, :]).then_inc(s_t2, 1)

            def bias3(t, k):
                act.wait_ge(s_m3, t * NG + (k + 1))
                act.wait_ge(s_m4, t * (NG // 2) + (k // 2 - 1))
                A(t3[k % 4][:, :, :], m3_ps, ACT.Identity, bias=bm3[:, :]).then_inc(s_t3, 1)

            def sdf(t):
                act.wait_ge(s_lim, t + 1)
                A(sg, sg, ACT.Exp, scale=-1.0).then_inc(s_e, 1)
                act.wait_ge(s_e, t + 1)
                A(sg, sg, ACT.Ln, bias=1.0).then_inc(s_le, 1)
                act.wait_ge(s_le, t + 1)
                A(sg, sg, ACT.Exp, scale=-1.0).then_inc(s_sg, 1)

            def layer1(t, pair, i, col, par, first, last):
                f_a, f_b, f_c = features(t + 1, 1 - par)
                for k in range(NG):
                    bias1(t, k, par)
                    if k >= 1:
                        bias2(t, k - 1)
                    elif not first:
                        bias2(t - 1, NG - 1)
                    if k >= 2:
                        bias3(t, k - 2)
                    elif k == 1 and not first:
                        bias3(t - 1, NG - 1)
                    elif k == 0 and not first:
                        bias3(t - 1, NG - 2)
                    if k == 2 and not first:
                        sdf(t - 1)
                    if not last:
                        if k == 3:
                            f_a()
                        if k == 5:
                            f_b()
                        if k == 7:
                            f_c()

            act.wait_ge(s_dve0, 1)
            with act.Fori(0, B) as b:
                t0 = fresh(act, b * T + 1)
                group_norm(b * 2)
                act.wait_ge(s_nb, b * 2 + 1)
                sq_, rs_, ez_, ec_, parts_, sp_ = prep(t0)
                sq_()
                rs_()
                ez_()
                ec_()
                parts_(0)
                sp_()
                walk(act, b, layer0)
                group_norm(b * 2 + 1)
                act.wait_ge(s_nb, b * 2 + 2)
                for f in features(fresh(act, b * T + 1), 0):
                    f()
                walk(act, b, layer1)
                t9 = fresh(act, b * T + T)
                bias2(t9, NG - 1)
                bias3(t9, NG - 2)
                bias3(t9, NG - 1)
                sdf(t9)

        @block.gpsimd
        def _(pool):
            chunk_zero(pool, pool_counts)

            def gate(t, par):
                pool.wait_ge(s_yv, t + 1)
                pool.wait_ge(s_sz, t + 1)
                nc.gpsimd.tensor_tensor(ex[:, :, :], ex[:, :, :], sz[par][:, :, :], ALU.mult).then_inc(s_gate, 1)

            def times_c(t, n):
                pool.wait_ge(s_Ccp, t * NS + (n + 1))
                pool.wait_ge(s_scan[0], t * NS + (n + 1))
                pool.wait_ge(s_scan[1], t * NS + (n + 1))
                pool.wait_ge(s_sum, t * NS + (n - 1))
                c = csb[n % 2][:, :].rearrange("p (o l) -> p o l", o=1).to_broadcast([P, 2, L])
                nc.gpsimd.tensor_tensor(ch[n % 2][:, :, :], H[:, n, :, :], c, ALU.mult).then_inc(s_ch, 1)

            def layer0(t, pair, i, col, par, first, last):
                for n in range(NS):
                    times_c(t, n)
                    if n == 1 and not first:
                        gate(t - 1, 1 - par)

            with pool.Fori(0, B) as b:
                walk(pool, b, layer0)
                gate(b * T + T, 1)

        @block.vector
        def _(dve):
            V = nc.vector
            chunk_zero(dve, dve_counts)
            dve.wait_ge(s_w, W_ALL)
            V.memset(epsc[:, :], EPS).then_inc(s_dve0, 1)
            win = w_x.rearrange("p (o n) -> p o n", o=1).to_broadcast([P, TAPS, 2 * P])
            V.tensor_tensor(w_conv[:, :, :, :].rearrange("p k h n -> p k (h n)"), tapw, win, ALU.mult).then_inc(s_dve0, 1)
            dve.wait_ge(s_act0, 1)
            V.tensor_scalar(a_neg[:, :, :], a_neg[:, :, :], -1.0, None, ALU.mult).then_inc(s_dve0, 1)
            dve.wait_ge(s_pe0, 2)
            V.tensor_copy(gw[:, :], ps[0:32, 0, 0:P]).then_inc(s_dve0, 1)
            V.tensor_tensor(gb[:, :], bm1[:, :], ps[:, 1, 0:1], ALU.add).then_inc(s_dve0, 1)
            dve.wait_ge(s_dve0, 5)
            V.tensor_scalar(ptb[:, :], pts[:, :], m1p[:, :], gb[:, :], ALU.mult, ALU.add).then_inc(s_dve0, 1)
            dve.wait_ge(s_dve0, 6)

            def group_norm(k):
                plain(dve)
                V.bn_aggr(mv[:, :], stats[:, :, :]).then_inc(s_mv, 1)
                dve.wait_ge(s_gm, k + 1)
                dve.wait_ge(s_mv, k + 1)
                V.tensor_tensor(dev[:, :], mv[:, 0:1], pp[:, 0, 0:1], ALU.subtract).then_inc(s_dev, 1)
                dve.wait_ge(s_dev, k + 1)
                V.scalar_tensor_tensor(out=vd[:, :], in0=dev[:, :], scalar=dev[:, :], in1=mv[:, 1:2],
                                       op0=ALU.mult, op1=ALU.add).then_inc(s_vd, 1)
                dve.wait_ge(s_gr, k + 1)
                V.scalar_tensor_tensor(out=gs[:, :], in0=pp[:, 0, 0:1], scalar=-1.0, in1=gr[:, :],
                                       op0=ALU.mult, op1=ALU.mult).then_inc(s_gs, 1)
                dve.wait_ge(s_cs, k + 1)

            def prep(t):
                def normed():
                    dve.wait_ge(s_rs, t + 1)
                    V.scalar_tensor_tensor(out=ln[:, :], in0=pp[:, 0, :], scalar=cs[:, :], in1=ln[:, :],
                                           op0=ALU.add, op1=ALU.mult).then_inc(s_xn, 1)

                def affine(carry):
                    dve.wait_ge(s_cv, t * 2)
                    dve.wait_ge(s_z, t)
                    if carry:
                        V.tensor_copy(xnf[:, 0:TAPS - 1], xnf[:, L:L + TAPS - 1]).then_inc(s_car, 1)
                    else:
                        V.memset(xnf[:, 0:TAPS - 1], 0.0).then_inc(s_car, 1)
                    dve.wait_ge(s_car, t + 1)
                    dve.wait_ge(s_xn, t + 1)
                    V.tensor_scalar(xnf[:, TAPS - 1:], ln[:, :], lnw[:, :], lnb[:, :], ALU.mult, ALU.add).then_inc(s_xnf, 1)

                def limit_z():
                    dve.wait_ge(s_z, t + 1)
                    V.tensor_scalar(ex[:, :, :], pp[:, :, :], SIGMOID_ZERO, None, ALU.max).then_inc(s_kz, 1)

                def silu_z(par):
                    dve.wait_ge(s_rz, t + 1)
                    V.tensor_tensor(sz[par][:, :, :], ex[:, :, :], pp[:, :, :], ALU.mult).then_inc(s_sz, 1)

                def limit_c():
                    dve.wait_ge(s_cv, t * 2 + 2)
                    for h in range(2):
                        m = V.tensor_scalar(ex[:, h, :], pp[:, h, :], cb[:, h:h + 1], SIGMOID_ZERO, ALU.add, ALU.max)
                    m.then_inc(s_kc, 1)

                def silu_c(par):
                    dve.wait_ge(s_rc, t + 1)
                    for h in range(2):
                        m = V.scalar_tensor_tensor(out=u[par][:, h, :], in0=pp[:, h, :], scalar=cb[:, h:h + 1],
                                                   in1=ex[:, h, :], op0=ALU.add, op1=ALU.mult)
                    m.then_inc(s_u, 1)

                def parts(par):
                    dve.wait_ge(s_hi, t + 1)
                    dve.wait_ge(s_xnf, t + 1)
                    dve.wait_ge(s_u, t + 1)
                    V.tensor_tensor(ln[0:96, :], pp[0:96, 0, :], bc[par][:, :], ALU.subtract).then_inc(s_rest, 1)
                    dve.wait_ge(s_rest, t + 1)
                    V.tensor_copy(bc[par][32:64, :], ln[32:64, :]).then_inc(s_mid, 1)
                    V.tensor_copy(mid, ln[64:96, :]).then_inc(s_mid, 1)
                    dve.wait_ge(s_mid, t * 2 + 2)
                    V.tensor_tensor(bc[par][64:96, :], ln[64:96, :], mid, ALU.subtract).then_inc(s_lo, 1)

                def clamp():
                    dve.wait_ge(s_dt, t + 1)
                    dve.wait_ge(s_lo, t + 1)
                    for h in range(2):
                        m = V.tensor_scalar(ex[:, h, :], pp[:, h, :], bdt[:, h:h + 1], SOFTPLUS_LINEAR, ALU.add, ALU.min)
                    m.then_inc(s_tm, 1)

                def steps(par):
                    dve.wait_ge(s_sp, t + 1)
                    dve.wait_ge(s_dA[1], t * NS)
                    dve.wait_ge(s_mulb, t * NS)
                    for h in range(2):
                        m = V.scalar_tensor_tensor(out=delta[:, h, :], in0=pp[:, h, :], scalar=bdt[:, h:h + 1],
                                                   in1=ex[:, h, :], op0=ALU.add, op1=ALU.max)
                    m.then_inc(s_del, 1)
                    dve.wait_ge(s_del, t + 1)
                    V.tensor_tensor(du[:, :, :], delta[:, :, :], u[par][:, :, :], ALU.mult).then_inc(s_du, 1)

                return normed, affine, limit_z, silu_z, limit_c, silu_c, parts, clamp, steps

            def times_b(t, n, par):
                dve.wait_ge(s_B, t * NS + (n + 1))
                dve.wait_ge(s_scan[1], t * NS + (n - 1))
                if n == 0:
                    dve.wait_ge(s_du, t + 1)
                bb = B_ps.rearrange("p (o l) -> p o l", o=1).to_broadcast([P, 2, L])
                V.tensor_tensor(dbu[n % 2][:, :, :], du[:, :, :], bb, ALU.mult).then_inc(s_mulb, 1)

            def scan(t, n):
                dve.wait_ge(s_mulb, t * NS + (n + 1))
                dve.wait_ge(s_ch, t * NS + (n + 1 - NS))
                for h in range(2):
                    dve.wait_ge(s_dA[h], t * NS + (n + 1))
                    V.tensor_tensor_scan(H[:, n, h, :], dA[:, h, :], dbu[n % 2][:, h, :], H[:, n, h, L - 1:L],
                                         ALU.mult, ALU.add).then_inc(s_scan[h], 1)

            def y_out(t, par):
                dve.wait_ge(s_sum, t * NS + NS)
                dve.wait_ge(s_o, t)
                for h in range(2):
                    m = V.scalar_tensor_tensor(out=ex[:, h, :], in0=u[par][:, h, :], scalar=dsk[:, h:h + 1],
                                               in1=y_ps[:, h, :], op0=ALU.mult, op1=ALU.add)
                m.then_inc(s_yv, 1)

            def residual(t, col, i):
                xc = X[:, bass.ds(col, L)]
                st = stats[:, bass.ds(i, 1), :].rearrange("p o s -> p (o s)")
                dve.wait_ge(s_o, t + 1)
                V.tensor_tensor(xc, xc, pp[:, 1, :], ALU.add).then_inc(s_res, 1)
                dve.wait_ge(s_res, t + 1)
                plain(dve)
                V.bn_stats(st, xc).then_inc(s_st1, 1)

            def layer0(t, pair, i, col, par, first, last):
                n_, a_, lz_, sz_, lc_, sc_, pa_, cl_, st_ = prep(t + 1)
                times_b(t, 0, par)
                for n in range(NS):
                    if n + 1 < NS:
                        times_b(t, n + 1, par)
                    scan(t, n)
                    if n == 1 and not first:
                        y_out(t - 1, 1 - par)
                    if n == 4 and not first:
                        residual(t - 1, col - L, i - 1)
                    if not last:
                        if n == 3:
                            n_()
                            a_(True)
                        if n == 5:
                            dve.wait_ge(s_o, t)
                            lz_()
                        if n == 7:
                            sz_(1 - par)
                        if n == 10:
                            lc_()
                        if n == 11:
                            sc_(1 - par)
                        if n == 12:
                            pa_(1 - par)
                        if n == 14:
                            cl_()
                        if n == 15:
                            st_(1 - par)

            def leaky(ap, s):
                V.scalar_tensor_tensor(out=ap, in0=ap, scalar=SLOPE, in1=ap, op0=ALU.mult, op1=ALU.max).then_inc(s, 1)

            def features(t):
                def first_layer():
                    dve.wait_ge(s_f1a, t + 1)
                    leaky(f1, s_f1l)

                def second_layer():
                    dve.wait_ge(s_f2a, t + 1)
                    leaky(f2, s_f2l)

                return first_layer, second_layer

            def flat(ap):
                return ap.rearrange("p k l -> p (k l)")

            def leaky1(t, k):
                dve.wait_ge(s_t1, t * NG + (k + 1))
                leaky(flat(t1[k % 2]), s_l1)

            def leaky2(t, k):
                dve.wait_ge(s_t2, t * (2 * NG) + (2 * k + 2))
                leaky(flat(t2[k % 2]), s_l2)

            def leaky3(t, k):
                dve.wait_ge(s_t3, t * NG + (k + 1))
                leaky(flat(t3[k % 4]), s_l3)

            def limit(t):
                dve.wait_ge(s_m4, t * (NG // 2) + NG // 2)
                dve.wait_ge(s_ob, t)
                V.tensor_scalar(sg, m4_ps, bm4[:, :], SIGMOID_ZERO, ALU.add, ALU.max).then_inc(s_lim, 1)

            def sdf(t, col, par):
                dve.wait_ge(s_sg, t + 1)
                V.tensor_tensor(ob[par], sg, X[:, bass.ds(col, L)], ALU.add).then_inc(s_ob, 1)

            def layer1(t, pair, i, col, par, first, last):
                f_a, f_b = features(t + 1)
                for k in range(NG):
                    leaky1(t, k)
                    if k >= 1:
                        leaky2(t, k - 1)
                    elif not first:
                        leaky2(t - 1, NG - 1)
                    if k >= 2:
                        leaky3(t, k - 2)
                    elif k == 1 and not first:
                        leaky3(t - 1, NG - 1)
                    elif k == 0 and not first:
                        leaky3(t - 1, NG - 2)
                    if k == 1 and not first:
                        limit(t - 1)
                    if k == 2 and not first:
                        if par == 1:
                            dve.wait_ge(s_out[0], pair * 16)
                        else:
                            dve.wait_ge(s_out[1], (pair - 1) * 16)
                        sdf(t - 1, col - L, 1 - par)
                    if not last:
                        if k == 3:
                            f_a()
                        if k == 5:
                            f_b()

            with dve.Fori(0, B) as b:
                t0 = fresh(dve, b * T + 1)
                dve.wait_ge(s_x, (b + 1) * (16 * XPARTS))
                for par in range(2):
                    dve.wait_ge(s_out[par], b * (16 * PAIRS) + 16)
                plain(dve)
                with dve.Fori(0, T) as i:
                    V.bn_stats(stats[:, bass.ds(i, 1), :].rearrange("p o s -> p (o s)"), X[:, bass.ds(i * L, L)]).then_inc(s_st, 1)
                dve.wait_ge(s_st, (b + 1) * T)
                group_norm(b * 2)
                V.tensor_scalar(cen_r[:, :], cen[:, :], gr[:, :], None, ALU.mult).then_inc(s_agg, 1)
                V.tensor_copy(cs[:, :], ps[:, 7, 0:1]).then_inc(s_h0, 1)
                V.memset(H[:, :, :, L - 1:L], 0.0).then_inc(s_h0, 1)
                dve.wait_ge(s_agg, b * 2 + 1)
                dve.wait_ge(s_h0, (b + 1) * 2)
                dve.sem_inc(s_nb, 1)
                n_, a_, lz_, sz_, lc_, sc_, pa_, cl_, st_ = prep(t0)
                n_()
                a_(False)
                lz_()
                sz_(0)
                lc_()
                sc_(0)
                pa_(0)
                cl_()
                st_(0)

                walk(dve, b, layer0)
                t9 = fresh(dve, b * T + T)
                y_out(t9, 1)
                residual(t9, (T - 1) * L, T - 1)
                dve.wait_ge(s_st1, t9 + 1)

                group_norm(b * 2 + 1)
                V.tensor_scalar(s1r[:, :], s1[:, :], gr[:, :], None, ALU.mult).then_inc(s_agg, 1)
                V.tensor_tensor(b1r[:, :], bs1[:, :], ps[0:64, 7, 0:1], ALU.add).then_inc(s_nw, 1)
                dve.wait_ge(s_agg, b * 2 + 2)
                dve.wait_ge(s_nw, b + 1)
                dve.sem_inc(s_nb, 1)
                for f in features(fresh(dve, b * T + 1)):
                    f()
                walk(dve, b, layer1)
                t9 = fresh(dve, b * T + T)
                leaky2(t9, NG - 1)
                leaky3(t9, NG - 2)
                leaky3(t9, NG - 1)
                limit(t9)
                dve.wait_ge(s_out[1], (b * PAIRS + PAIRS) * 16)
                sdf(t9, (T - 1) * L, 1)


def kernel(**inputs):
    import numpy as np
    import concourse.bacc as bacc
    import ml_dtypes
    from concourse import mybir as mb
    from concourse.bass_utils import run_bass_kernel_spmd as run

    q = {k: np.ascontiguousarray(v) for k, v in inputs.items()}
    B, C, Hh, Ww = q["x"].shape
    f = np.float32

    def halves(a):
        return np.ascontiguousarray(a.reshape(2, P, -1).transpose(1, 0, 2))

    def col(a):
        return np.ascontiguousarray(a.reshape(-1, 1))

    xp_t = q["L0_conv_W_xproj"].T
    xp_t = np.concatenate([xp_t[:, DTR:]] * 3 + [xp_t[:, :DTR]], axis=1)
    mw1, mw2, mw3, mw4 = (q[f"L1_conv_mw{i}"] for i in (1, 2, 3, 4))
    mw2_bd = np.zeros((P, P), f)
    mw3_bd = np.zeros((P, 64), f)
    mw4_bd = np.zeros((P, 4, 32), f)
    for j in range(4):
        mw2_bd[32 * j:32 * j + 32, 32 * j:32 * j + 32] = mw2.T
        mw3_bd[32 * j:32 * j + 32, 16 * j:16 * j + 16] = mw3.T
    for k in range(4):
        for j in range(8):
            mw4_bd[16 * j:16 * j + 16, k, 8 * k + j] = mw4[0]
    eye = np.eye(P, dtype=f)
    c = np.arange(P)
    gm = ((c[:, None] // 4) == (c[None, :] // 4)).astype(f) / 4
    om = np.full((P, P), 1.0 / P, f)
    pick = np.zeros((96, 2 * NS, P), ml_dtypes.bfloat16)
    for k in range(96):
        pick[k, k % 32, :] = 1
    lin = np.linspace(-1.0, 1.0, P, dtype=f)
    points = np.zeros((P, NG * GQ), f)
    for quad in range(NG * GQ):
        s, e = quad // 2, quad % 2
        for j in range(4):
            points[32 * j:32 * j + 32, quad] = lin[32 * (s % 4) + 8 * (s // 4) + 4 * e + j]

    arrays = dict(
        x=q["x"].reshape(B, C, Hh * Ww),
        w_in_t=np.ascontiguousarray(q["L0_conv_W_in"].T),
        conv_w_t=np.ascontiguousarray(q["L0_conv_conv_w"].T),
        conv_b=halves(q["L0_conv_conv_b"].reshape(-1, 1))[:, :, 0],
        ln_w=col(q["L0_conv_ln_w"]), ln_b=col(q["L0_conv_ln_b"]),
        w_xproj_t=halves(xp_t),
        w_dt_t=np.ascontiguousarray(q["L0_conv_W_dt"].T.reshape(DTR, 2, P)),
        b_dt=halves(q["L0_conv_b_dt"].reshape(-1, 1))[:, :, 0],
        a_log=halves(q["L0_conv_A_log"]),
        d_skip=halves(q["L0_conv_D"].reshape(-1, 1))[:, :, 0],
        w_out_t=halves(q["L0_conv_W_out"].T),
        sw1_t=q["L1_conv_sw1"].T, sb1=col(q["L1_conv_sb1"]), sw2_t=q["L1_conv_sw2"].T, sb2=col(q["L1_conv_sb2"]),
        sw3=q["L1_conv_sw3"], sb3=col(q["L1_conv_sb3"]),
        mw1_t=np.tile(mw1[:, :16].T, (1, 4)), mw1_pt=col(np.tile(mw1[:, 16], 4)), mb1=col(np.tile(q["L1_conv_mb1"], 4)),
        mw2_bd=mw2_bd, mb2=col(np.tile(q["L1_conv_mb2"], 4)), mw3_bd=mw3_bd, mb3=col(np.tile(q["L1_conv_mb3"], 8)),
        mw4_bd=mw4_bd, mb4=col(np.tile(q["L1_conv_mb4"], P)),
        center=eye - om, group_mean=gm, ones_mean=om, ident=eye, pick=pick, points=points,
    )
    nc = bacc.Bacc("TRN2", target_bir_lowering=False, num_devices=1)
    feed, args = {}, []
    for name, a in arrays.items():
        a = np.ascontiguousarray(a)
        feed["in_" + name] = a
        args.append(nc.dram_tensor("in_" + name, a.shape, mb.dt.from_np(a.dtype), kind="ExternalInput").ap())
    out = nc.dram_tensor("out", (B, C, Hh * Ww), mb.dt.float32, kind="ExternalOutput").ap()
    mamba_sdf_kernel(nc, *args, out)
    r = run(nc, [feed], core_ids=[0])
    return r.results[0]["out"].reshape(B, C, Hh, Ww)
```

```python
from contextlib import ExitStack

import concourse.bass as bass
from concourse import mybir

F32 = mybir.dt.float32
BF16 = mybir.dt.bfloat16
ALU = mybir.AluOpType
ACT = mybir.ActivationFunctionType

P = 128
L = 512
NS = 16
TAPS = 4
DTR = 8
HR = 8
CR = 4
LAG = 3
GQ = 4
NG = 8
SLOPE = 0.01
SOFTPLUS_LINEAR = 20.0
SIGMOID_ZERO = -44.0
EPS = 1e-5


def mamba_sdf_kernel(nc, x, w_in_t, conv_w_t, conv_b, ln_w, ln_b, w_xproj_t, w_dt_t, b_dt, a_log,
                     d_skip, w_out_t, sw1_t, sb1, sw2_t, sb2, sw3, sb3, mw1_t, mw1_pt, mb1, mw2_bd, mb2,
                     mw3_bd, mb3, mw4_bd, mb4, center, group_mean, ones_mean, ident, pick, points, out):
    B, _, N = x.shape
    T = N // L
    PAIRS = T // 2

    with ExitStack() as ctx:
        def sb(name, shape, dt=F32):
            return ctx.enter_context(nc.sbuf_tensor(name, shape, dt))

        def sem(name):
            return ctx.enter_context(nc.semaphore(name))

        w_z = sb("w_z", [P, 2 * P])
        w_conv = sb("w_conv", [P, TAPS, 2, P])
        cb = sb("cb", [P, 2])
        lnw = sb("lnw", [P, 1])
        lnb = sb("lnb", [P, 1])
        w_xp = sb("w_xp", [P, 2, 104])
        w_dt = sb("w_dt", [104, 2, P])
        bdt = sb("bdt", [P, 2])
        a_neg = sb("a_neg", [P, 2, NS])
        dsk = sb("dsk", [P, 2])
        w_out = sb("w_out", [P, 2, P])
        cen = sb("cen", [P, P])
        gmean = sb("gmean", [P, P])
        omean = sb("omean", [P, 1])
        idn = sb("idn", [P, P])
        pk = sb("pk", [96, 2 * NS], BF16)
        s1 = sb("s1", [P, 64])
        bs1 = sb("bs1", [64, 1])
        s2 = sb("s2", [64, 32])
        bs2 = sb("bs2", [32, 1])
        s3 = sb("s3", [16, 32])
        bs3 = sb("bs3", [16, 1])
        m1 = sb("m1", [16, P])
        m1p = sb("m1p", [P, 1])
        bm1 = sb("bm1", [P, 1])
        m2 = sb("m2", [P, P])
        bm2 = sb("bm2", [P, 1])
        m3 = sb("m3", [P, 64])
        bm3 = sb("bm3", [P, 1])
        bm3s = sb("bm3s", [P, 2])
        m4 = sb("m4", [P, 4, 32])
        bm4 = sb("bm4", [P, 1])
        pts = sb("pts", [P, NG * GQ])
        ptb = sb("ptb", [P, NG * GQ])
        gw = sb("gw", [32, P])
        gb = sb("gb", [P, 1])
        epsc = sb("epsc", [P, 1])

        X = sb("X", [P, N])
        stats = sb("stats", [P, T, 6])
        mv = sb("mv", [P, 2])
        dev = sb("dev", [P, 1])
        vd = sb("vd", [P, 1])
        lnv = sb("lnv", [P, 1])
        gr = sb("gr", [P, 1])
        gs = sb("gs", [P, 1])
        cen_r = sb("cen_r", [P, P])
        cs = sb("cs", [P, 1])
        s1r = sb("s1r", [P, 64])
        b1r = sb("b1r", [64, 1])

        arena = sb("arena", [P, 55 * L])

        def over(k, n):
            return arena[:, k * L:(k + n) * L]

        def halves(k):
            return over(k, 2).rearrange("p (h l) -> p h l", h=2)

        H = over(0, 2 * HR).rearrange("p (n h l) -> p n h l", n=HR, h=2)
        ch = [halves(16 + 2 * i) for i in range(CR)]
        csb = [over(24 + i, 1) for i in range(CR)]
        dbu = [halves(28 + 2 * i) for i in range(2)]
        dA = [halves(32 + 2 * i) for i in range(2)]
        delta = [halves(36 + 2 * i) for i in range(2)]
        du = [halves(40 + 2 * i) for i in range(2)]
        u = [halves(44 + 2 * i) for i in range(2)]
        sz = [halves(48 + 2 * i) for i in range(2)]
        yo = halves(52)
        exz = over(54, 1)
        carried = sb("carried", [P, NS, 2])
        bc = [sb(f"bc{i}", [96, L], BF16) for i in range(2)]
        ln = sb("ln", [P, L])
        dts = ln
        xnf = sb("xnf", [P, TAPS - 1 + L])
        ex = sb("ex", [P, 2, L])
        mid = ex[64:96, 0, 0:L // 2].bitcast(BF16)
        w_x = csb[0][:, 0:2 * P]
        tapw = over(16, 2).rearrange("p (k n) -> p k n", n=2 * P)

        t1 = [over(4 * i, 4).rearrange("p (k l) -> p k l", k=GQ) for i in range(4)]
        t2 = [over(16 + 4 * i, 4).rearrange("p (k l) -> p k l", k=GQ) for i in range(4)]
        t3 = [over(32 + 2 * i, 2).rearrange("p (k l) -> p k l", k=2) for i in range(4)]
        t3s = [over(47 + 2 * i, 2).rearrange("p (k l) -> p k l", k=2) for i in range(2)]
        g = [over(40 + i, 1) for i in range(2)]
        f1 = over(42, 1)[0:64]
        f2 = over(43, 1)[0:32]
        sg = over(44, 1)
        ob = [over(45 + i, 1) for i in range(2)]

        ps = ctx.enter_context(nc.psum_tensor("ps", [P, 8, L], F32))
        y_ps, pp = ps[:, 0:2, :], ps[:, 2:4, :]
        B_ps, C_ps, qp = [ps[:, 4, :], ps[:, 5, :]], ps[:, 6, :], ps[:, 7, :]
        m2_ps = [ps[:, 0:2, :], ps[:, 4:6, :]]
        m3_ps = ps[:, 6:8, :]
        m4_ps, f_ps = ps[:, 2, :], ps[:, 3, :]

        s_w = sem("s_weights_loaded")
        s_act0, s_dve0, s_pe0 = sem("s_act_setup"), sem("s_dve_setup"), sem("s_pe_setup")
        s_x = sem("s_x_loaded")
        s_carry = sem("s_carry_wait")
        s_mv, s_gm, s_vd, s_gv = sem("s_mean_var"), sem("s_group_mean"), sem("s_group_dev"), sem("s_group_var")
        s_dev, s_lnv, s_gr, s_gs = sem("s_dev"), sem("s_log_var"), sem("s_group_rstd"), sem("s_group_shift")
        s_nw, s_cs, s_nb = sem("s_norm_weights"), sem("s_shift_product"), sem("s_norm_bias")
        s_st, s_agg, s_h0 = sem("s_stats"), sem("s_aggregated"), sem("s_state_cleared")
        s_last = sem("s_last_copied")
        s_cen, s_sq, s_var, s_lv, s_rs = sem("s_centered"), sem("s_squared"), sem("s_variance"), sem("s_logvar"), sem("s_rstd")
        s_xn, s_car, s_xnf = sem("s_normed"), sem("s_carried"), sem("s_affine")
        s_z, s_kz, s_ez, s_lz, s_rz, s_sz = sem("s_z"), sem("s_limited_z"), sem("s_exp_z"), sem("s_log_z"), sem("s_sigmoid_z"), sem("s_silu_z")
        s_cv, s_kc, s_ec, s_lc, s_rc, s_u = sem("s_conv"), sem("s_limited_c"), sem("s_exp_c"), sem("s_log_c"), sem("s_sigmoid_c"), sem("s_u")
        s_xd, s_hi, s_dts, s_rest, s_mid, s_lo = sem("s_xdbl"), sem("s_bc_high"), sem("s_dt_copied"), sem("s_bc_rest"), sem("s_bc_mid"), sem("s_bc_low")
        s_dt, s_tm, s_ed, s_sp, s_del, s_du = sem("s_dt"), sem("s_clamped"), sem("s_exp_dt"), sem("s_log_dt"), sem("s_delta"), sem("s_delta_u")
        s_B, s_C, s_mulb, s_dA0, s_dA1 = sem("s_B_spread"), sem("s_C_spread"), sem("s_dBu"), sem("s_decay0"), sem("s_decay1")
        s_dA = [s_dA0, s_dA1]
        s_scan = [sem("s_scan0"), sem("s_scan1")]
        s_Ccp, s_ch, s_sum = sem("s_C_copied"), sem("s_Ch"), sem("s_summed")
        s_yv, s_gate, s_o, s_res, s_st1 = sem("s_y_out"), sem("s_gated"), sem("s_projected"), sem("s_residual"), sem("s_stats1")
        s_f1, s_f1a, s_f1l = sem("s_f1"), sem("s_f1_biased"), sem("s_f1_relu")
        s_f2, s_f2a, s_f2l = sem("s_f2"), sem("s_f2_biased"), sem("s_f2_relu")
        s_gp, s_g = sem("s_g_product"), sem("s_g")
        s_t1, s_t1p, s_l1, s_m2 = sem("s_h1_biased"), sem("s_h1_biased_last"), sem("s_h1"), sem("s_mm2")
        s_t2, s_l2, s_m3 = sem("s_h2_biased"), sem("s_h2"), sem("s_mm3")
        s_t3, s_l3, s_m4 = sem("s_h3_biased"), sem("s_h3"), sem("s_mm4")
        s_lim = sem("s_sdf_limited")
        s_e, s_le, s_sg, s_ob, s_out = sem("s_sdf_exp"), sem("s_sdf_log"), sem("s_sdf"), sem("s_out_ready"), [sem("s_out_stored0"), sem("s_out_stored1")]

        pe_counts = {s_cen: 1, s_var: 1, s_z: 2, s_cv: 2, s_xd: 1, s_dt: 1, s_B: NS, s_C: NS, s_sum: NS, s_o: 1,
                     s_f1: 1, s_f2: 1, s_gp: 1, s_m2: 2 * NG, s_m3: NG, s_m4: NG // 2}
        act_counts = {s_sq: 1, s_lv: 1, s_rs: 1, s_ez: 2, s_lz: 2, s_rz: 2, s_ec: 1, s_lc: 1, s_rc: 1, s_hi: 1, s_dts: 1,
                      s_ed: 1, s_sp: 1, s_dA0: NS, s_dA1: NS, s_Ccp: NS, s_f1a: 1, s_f2a: 1, s_g: 1,
                      s_t1: NG, s_t2: 2 * NG, s_t3: NG, s_e: 1, s_le: 1, s_sg: 1}
        pool_counts = {s_ch: NS, s_gate: 1, s_t1p: NG, s_l3: NG}
        dve_counts = {s_xn: 1, s_car: 1, s_xnf: 1, s_kz: 2, s_sz: 2, s_last: NS // 4, s_kc: 1, s_u: 1, s_rest: 1, s_mid: 2, s_lo: 1,
                      s_tm: 1, s_del: 1, s_du: 1, s_mulb: NS, s_scan[0]: NS, s_scan[1]: NS, s_yv: 1, s_res: 1, s_st1: 1,
                      s_f1l: 1, s_f2l: 1, s_l1: NG, s_l2: NG, s_lim: 1, s_ob: 1}

        def chunk_zero(eng, counts):
            for s, n in counts.items():
                eng.sem_inc(s, n)

        loads = [
            (w_x, w_in_t[:, 0:2 * P]), (w_z[:], w_in_t[:, 2 * P:4 * P]), (tapw, conv_w_t.partition_broadcast(P)), (cb[:], conv_b), (lnw[:], ln_w), (lnb[:], ln_b),
            (w_xp[:], w_xproj_t), (w_dt[96:104], w_dt_t), (bdt[:], b_dt), (a_neg[:], a_log), (dsk[:], d_skip),
            (w_out[:], w_out_t), (cen[:], center), (gmean[:], group_mean), (omean[:], ones_mean), (idn[:], ident),
            (pk[:], pick), (s1[:], sw1_t), (bs1[:], sb1), (s2[:], sw2_t), (bs2[:], sb2), (s3[:], sw3), (bs3[:], sb3),
            (m1[:], mw1_t), (m1p[:], mw1_pt), (bm1[:], mb1), (m2[:], mw2_bd), (bm2[:], mb2), (m3[:], mw3_bd),
            (bm3[:], mb3), (m4[:], mw4_bd), (bm4[:], mb4), (pts[:], points),
        ]
        W_ALL = 16 * len(loads)
        XPARTS = 8

        def fresh(eng, value):
            return eng.snap(eng.to_reg(value))

        def plain(eng):
            eng.sem_inc(s_carry, 1)

        def walk(eng, b, chunk):
            for par in range(2):
                chunk(fresh(eng, b * T + (1 + par)), fresh(eng, b * PAIRS + 1), par, par * L, par, par == 0, False)
            with eng.Fori(1, PAIRS - 1) as j:
                for par in range(2):
                    chunk(fresh(eng, b * T + j * 2 + (1 + par)), fresh(eng, b * PAIRS + j + 1), j * 2 + par,
                          fresh(eng, j * (2 * L) + par * L), par, False, False)
            for par in range(2):
                i = T - 2 + par
                chunk(fresh(eng, b * T + (i + 1)), fresh(eng, b * PAIRS + PAIRS), i, i * L, par, False, par == 1)

        block = ctx.enter_context(nc.Block())

        @block.sync
        def _(sp):
            chunk_zero(sp, {s_out[0]: 16, s_out[1]: 16})
            for dst, src in loads:
                sp.dma_start(dst, src).then_inc(s_w, 16)
            with sp.Fori(0, B) as b:
                sp.wait_ge(s_ob, b * T + 1)
                for k in range(XPARTS):
                    w = N // XPARTS
                    sp.dma_start(X[:, k * w:(k + 1) * w], x[b, :, k * w:(k + 1) * w]).then_inc(s_x, 16)

                def chunk(t, pair, i, col, par, first, last):
                    sp.wait_ge(s_ob, t + 1)
                    sp.dma_start(out[b, :, bass.ds(col, L)], ob[par]).then_inc(s_out[par], 16)

                walk(sp, b, chunk)
            for par in range(2):
                sp.wait_ge(s_out[par], 16 * (B * PAIRS + 1))

        @block.tensor
        def _(pe):
            mm = nc.tensor.matmul
            chunk_zero(pe, pe_counts)

            pe.wait_ge(s_w, W_ALL)
            mm(ps[0:32, 0, 0:P], s3[:, :], m1[:, :], start=True, stop=True).then_inc(s_pe0, 1)
            mm(ps[:, 1, 0:1], m1[:, :], bs3[:, :], start=True, stop=True).then_inc(s_pe0, 1)

            def group_norm(k, weights, width):
                pe.wait_ge(s_mv, k + 1)
                mm(pp[:, 0, 0:1], gmean[:, :], mv[:, 0:1], start=True, stop=True).then_inc(s_gm, 1)
                pe.wait_ge(s_vd, k + 1)
                mm(pp[:, 1, 0:1], gmean[:, :], vd[:, :], start=True, stop=True).then_inc(s_gv, 1)
                pe.wait_ge(s_gs, k + 1)
                mm(ps[0:width, 7, 0:1], weights, gs[:, :], start=True, stop=True).then_inc(s_cs, 1)

            def prep(t, col):
                def center_it():
                    pe.wait_ge(s_del, t)
                    mm(pp[:, 0, :], cen_r[:, :], X[:, bass.ds(col, L)], start=True, stop=True).then_inc(s_cen, 1)

                def variance():
                    pe.wait_ge(s_sq, t + 1)
                    mm(pp[:, 1, :], omean[:, :].to_broadcast([P, P]), ln[:, :], start=True, stop=True).then_inc(s_var, 1)

                def z(h, start=False):
                    pe.wait_ge(s_xnf, t + 1)
                    if not start:
                        pe.wait_ge(s_res, t - 1)
                    pe.wait_ge(s_sz, t * 2 + h)
                    mm(qp, w_z[:, h * P:(h + 1) * P], xnf[:, TAPS - 1:], start=True, stop=True).then_inc(s_z, 1)

                def conv(h, a):
                    if h == 0 and a == 0:
                        pe.wait_ge(s_xnf, t + 1)
                        pe.wait_ge(s_lv, t + 1)
                    for k in range(a, a + 2):
                        m = mm(pp[:, h, :], w_conv[:, k, h, :], xnf[:, k:k + L], start=k == 0, stop=k == TAPS - 1)
                    if a == 2:
                        m.then_inc(s_cv, 1)

                def xdbl():
                    pe.wait_ge(s_u, t + 1)
                    for h in range(2):
                        m = mm(pp[0:104, 0, :], w_xp[:, h, :], u_of(t)[:, h, :], start=h == 0, stop=h == 1)
                    m.then_inc(s_xd, 1)

                def step_size():
                    pe.wait_ge(s_dts, t + 1)
                    pe.wait_ge(s_rest, t + 1)
                    for h in range(2):
                        m = mm(pp[:, h, :], w_dt[96:104, h, :], dts[96:104, :], start=True, stop=True)
                    m.then_inc(s_dt, 1)

                return center_it, variance, z, conv, xdbl, step_size

            par_now = [0]

            def u_of(t):
                return u[par_now[0]]

            def spread_b(t, n, par):
                if n == 0:
                    pe.wait_ge(s_lo, t + 1)
                pe.wait_ge(s_mulb, t * NS + (n - 1))
                mm(B_ps[n % 2], pk[:, n:n + 1].to_broadcast([96, P]), bc[par][:, :], start=True, stop=True).then_inc(s_B, 1)

            def spread_c(t, n, par):
                pe.wait_ge(s_Ccp, t * NS + n)
                mm(C_ps, pk[:, NS + n:NS + n + 1].to_broadcast([96, P]), bc[par][:, :], start=True, stop=True).then_inc(s_C, 1)

            def add_state(t, n):
                if n == 0:
                    pe.wait_ge(s_yv, t)
                pe.wait_ge(s_ch, t * NS + (n + 1))
                for h in range(2):
                    m = mm(y_ps[:, h, :], idn[:, :], ch[n % CR][:, h, :], start=n == 0, stop=n == NS - 1)
                m.then_inc(s_sum, 1)

            def project_out(t, z_ahead):
                pe.wait_ge(s_gate, t + 1)
                pe.wait_ge(s_sz, t * 2 + (4 if z_ahead else 2))
                for h in range(2):
                    m = mm(qp, w_out[:, h, :], yo[:, h, :], start=h == 0, stop=h == 1)
                m.then_inc(s_o, 1)

            def layer0(t, pair, i, col, par, first, last):
                par_now[0] = 1 - par
                if not last:
                    cen_, var_, z_, conv_, xd_, dt_ = prep(t + 1, col + L)
                for n in range(NS):
                    if n + 2 < NS:
                        spread_b(t, n + 2, par)
                    elif not last:
                        spread_b(t + 1, n + 2 - NS, 1 - par)
                    if n + 1 < NS:
                        spread_c(t, n + 1, par)
                    elif not last:
                        spread_c(t + 1, 0, 1 - par)
                    if not last:
                        if n == 0:
                            cen_()
                        if n == 1:
                            var_()
                    if n < LAG:
                        if not first:
                            add_state(t - 1, NS - LAG + n)
                    elif n == 4:
                        add_state(t, 0)
                    elif n == 5:
                        add_state(t, 1)
                        add_state(t, 2)
                    elif n > 5:
                        add_state(t, n - LAG)
                    if n == 6 and not first:
                        project_out(t - 1, True)
                    if not last:
                        if 3 <= n <= 6:
                            conv_((n - 3) // 2, 2 * ((n - 3) % 2))
                        if n in (8, 11):
                            z_((n - 8) // 3)
                        if n == 10:
                            xd_()
                        if n == 12:
                            dt_()

            def layer0_start(t):
                par_now[0] = 0
                cen_, var_, z_, conv_, xd_, dt_ = prep(t, 0)
                cen_()
                var_()
                for h in range(2):
                    for a in (0, 2):
                        conv_(h, a)
                z_(0, True)
                xd_()
                z_(1, True)
                dt_()
                spread_b(t, 0, 0)
                spread_b(t, 1, 0)
                spread_c(t, 0, 0)

            def layer0_end(t):
                for n in range(NS - LAG, NS):
                    add_state(t, n)
                project_out(t, False)

            def features(t, col, par):
                def first_layer():
                    pe.wait_ge(s_g, t)
                    mm(f_ps[0:64], s1r[:, :], X[:, bass.ds(col, L)], start=True, stop=True).then_inc(s_f1, 1)

                def second_layer():
                    pe.wait_ge(s_f1l, t + 1)
                    plain(pe)
                    mm(f_ps[0:32], s2[:, :], f1, start=True, stop=True).then_inc(s_f2, 1)

                def third_layer():
                    pe.wait_ge(s_f2l, t + 1)
                    mm(f_ps, gw[:, :], f2, start=True, stop=True).then_inc(s_gp, 1)

                return first_layer, second_layer, third_layer

            def mm2(t, k):
                pe.wait_ge(s_l1, t * NG + (k + 1))
                for half in range(2):
                    pe.wait_ge(s_t2, t * (2 * NG) + (2 * k + half - 1))
                    for j in range(2):
                        q = 2 * half + j
                        m = mm(m2_ps[half][:, j, :], m2[:, :], t1[k % 4][:, q, :], start=True, stop=True)
                    m.then_inc(s_m2, 1)

            def mm3(t, k):
                pe.wait_ge(s_l2, t * NG + (k + 1))
                pe.wait_ge(s_t3, t * NG + k)
                for s in range(2):
                    for e in range(2):
                        m = mm(m3_ps[64 * e:64 * e + 64, s, :], m3[:, :], t2[k % 4][:, 2 * s + e, :],
                               start=True, stop=True)
                m.then_inc(s_m3, 1)

            def mm4(t, k):
                pe.wait_ge(s_l3, t * NG + (k + 1))
                if k == 1:
                    pe.wait_ge(s_lim, t)
                for quadrant in range(4):
                    m = mm(m4_ps[32 * quadrant:32 * quadrant + 32, :], m4[:, k // 2, :],
                           t3[(k - 1 + quadrant // 2) % 4][:, quadrant % 2, :], start=k == 1, stop=k == NG - 1)
                m.then_inc(s_m4, 1)

            def layer1(t, pair, i, col, par, first, last):
                f_a, f_b, f_c = features(t + 1, col + L, 1 - par)
                for k in range(NG):
                    mm2(t, k)
                    if k >= 2:
                        mm3(t, k - 2)
                    elif not first:
                        mm3(t - 1, NG - 2 + k)
                    if k in (5, 7):
                        mm4(t, k - 4)
                    if k in (1, 3) and not first:
                        mm4(t - 1, NG - 4 + k)
                    if not last:
                        if k == 0:
                            f_a()
                        if k == 2:
                            f_b()
                        if k == 4:
                            f_c()

            with pe.Fori(0, B) as b:
                t0 = fresh(pe, b * T + 1)
                pe.wait_ge(s_w, W_ALL)
                group_norm(b * 2, cen[:, :], P)
                pe.wait_ge(s_nb, b * 2 + 1)
                layer0_start(t0)
                walk(pe, b, layer0)
                layer0_end(fresh(pe, b * T + T))
                group_norm(b * 2 + 1, s1[:, :], 64)
                pe.wait_ge(s_nb, b * 2 + 2)
                plain(pe)
                for f in features(fresh(pe, b * T + 1), 0, 0):
                    f()
                walk(pe, b, layer1)
                t9 = fresh(pe, b * T + T)
                mm3(t9, NG - 2)
                mm3(t9, NG - 1)
                mm4(t9, NG - 3)
                mm4(t9, NG - 1)

        @block.scalar
        def _(act):
            A = nc.scalar.activation
            chunk_zero(act, act_counts)
            nc.scalar.preload_act_table_set("natural_log_exp_and_others")
            act.wait_ge(s_w, W_ALL)
            A(a_neg[:, :, :], a_neg[:, :, :], ACT.Exp).then_inc(s_act0, 1)

            def group_norm(k):
                act.wait_ge(s_gv, k + 1)
                A(lnv[:, :], pp[:, 1, 0:1], ACT.Ln, bias=epsc[:, :]).then_inc(s_lnv, 1)
                act.wait_ge(s_lnv, k + 1)
                A(gr[:, :], lnv[:, :], ACT.Exp, scale=-0.5).then_inc(s_gr, 1)

            def prep(t):
                def square():
                    act.wait_ge(s_cen, t + 1)
                    act.wait_ge(s_lo, t)
                    act.wait_ge(s_dt, t)
                    A(ln[:, :], pp[:, 0, :], ACT.Square, bias=cs[:, :]).then_inc(s_sq, 1)

                def rstd():
                    act.wait_ge(s_var, t + 1)
                    A(ln[:, :], pp[:, 1, :], ACT.Ln, bias=epsc[:, :]).then_inc(s_lv, 1)
                    act.wait_ge(s_lv, t + 1)
                    A(ln[:, :], ln[:, :], ACT.Exp, scale=-0.5).then_inc(s_rs, 1)

                def sigmoid(v, count, limited, exp, log, done):
                    act.wait_ge(limited, count)
                    A(v, v, ACT.Exp, scale=-1.0).then_inc(exp, 1)
                    act.wait_ge(exp, count)
                    A(v, v, ACT.Ln, bias=1.0).then_inc(log, 1)
                    act.wait_ge(log, count)
                    A(v, v, ACT.Exp, scale=-1.0).then_inc(done, 1)

                def sigmoid_z(h):
                    sigmoid(exz, t * 2 + (h + 1), s_kz, s_ez, s_lz, s_rz)

                def sigmoid_c():
                    sigmoid(ex[:, :, :], t + 1, s_kc, s_ec, s_lc, s_rc)

                def parts(par):
                    act.wait_ge(s_xd, t + 1)
                    A(bc[par][:, :], pp[0:96, 0, :], ACT.Copy).then_inc(s_hi, 1)
                    act.wait_ge(s_dt, t)
                    A(dts[96:104, :], pp[96:104, 0, :], ACT.Copy).then_inc(s_dts, 1)

                def softplus():
                    act.wait_ge(s_tm, t + 1)
                    A(ex[:, :, :], ex[:, :, :], ACT.Exp).then_inc(s_ed, 1)
                    act.wait_ge(s_ed, t + 1)
                    A(ex[:, :, :], ex[:, :, :], ACT.Ln, bias=1.0).then_inc(s_sp, 1)

                return square, rstd, sigmoid_z, sigmoid_c, parts, softplus

            def decay(t, n, par):
                if n == 0:
                    act.wait_ge(s_del, t + 1)
                for h in range(2):
                    act.wait_ge(s_scan[h], t * NS + (n - 1))
                    A(dA[n % 2][:, h, :], delta[par][:, h, :], ACT.Exp, scale=a_neg[:, h, n:n + 1]).then_inc(s_dA[h], 1)

            def copy_c(t, n):
                act.wait_ge(s_C, t * NS + (n + 1))
                act.wait_ge(s_ch, t * NS + (n + 1 - CR))
                A(csb[n % CR], C_ps, ACT.Copy).then_inc(s_Ccp, 1)

            def layer0(t, pair, i, col, par, first, last):
                sq_, rs_, ez_, ec_, parts_, sp_ = prep(t + 1)
                for n in range(NS):
                    if n + 1 < NS:
                        decay(t, n + 1, par)
                        copy_c(t, n + 1)
                    elif not last:
                        decay(t + 1, 0, 1 - par)
                        copy_c(t + 1, 0)
                    if not last:
                        if n == 0:
                            sq_()
                        if n == 1:
                            rs_()
                        if n == 8:
                            ec_()
                        if n in (9, 12):
                            ez_((n - 9) // 3)
                        if n == 10:
                            parts_(1 - par)
                        if n == 13:
                            sp_()

            def features(t, par):
                def first_layer():
                    act.wait_ge(s_f1, t + 1)
                    act.wait_ge(s_f2, t)
                    A(f1, f_ps[0:64], ACT.Identity, bias=b1r[:, :]).then_inc(s_f1a, 1)

                def second_layer():
                    act.wait_ge(s_f2, t + 1)
                    act.wait_ge(s_gp, t)
                    A(f2, f_ps[0:32], ACT.Identity, bias=bs2[:, :]).then_inc(s_f2a, 1)

                def third_layer():
                    act.wait_ge(s_gp, t + 1)
                    A(g[par], f_ps, ACT.Copy).then_inc(s_g, 1)

                return first_layer, second_layer, third_layer

            def bias1(t, k, par):
                if k == 0:
                    act.wait_ge(s_g, t + 1)
                act.wait_ge(s_m2, t * (2 * NG) + 2 * (k - 3))
                for q in range(GQ - 2):
                    m = A(t1[k % 4][:, q, :], g[par], ACT.Identity, bias=ptb[:, GQ * k + q:GQ * k + q + 1])
                m.then_inc(s_t1, 1)

            def bias2(t, k, half):
                act.wait_ge(s_m2, t * (2 * NG) + (2 * k + half + 1))
                if half == 0:
                    act.wait_ge(s_m3, t * NG + (k - 3))
                A(t2[k % 4][:, 2 * half:2 * half + 2, :], m2_ps[half], ACT.Identity, bias=bm2[:, :]).then_inc(s_t2, 1)

            def bias3(t, k):
                act.wait_ge(s_m3, t * NG + (k + 1))
                act.wait_ge(s_m4, t * (NG // 2) + (k // 2 - 1))
                act.wait_ge(s_l3, t * NG + (k - 1))
                A(t3[k % 4], m3_ps, ACT.Relu, bias=bm3s[:, 1:2], scale=1 - SLOPE)
                A(t3s[k % 2], m3_ps, ACT.Identity, bias=bm3s[:, 0:1], scale=SLOPE).then_inc(s_t3, 1)

            def sdf(t):
                act.wait_ge(s_lim, t + 1)
                A(sg, sg, ACT.Exp, scale=-1.0).then_inc(s_e, 1)
                act.wait_ge(s_e, t + 1)
                A(sg, sg, ACT.Ln, bias=1.0).then_inc(s_le, 1)
                act.wait_ge(s_le, t + 1)
                A(sg, sg, ACT.Exp, scale=-1.0).then_inc(s_sg, 1)

            def layer1(t, pair, i, col, par, first, last):
                f_a, f_b, f_c = features(t + 1, 1 - par)
                for k in range(NG):
                    bias2(t, k, 0)
                    nxt = (t, k + 2, par) if k + 2 < NG else (t + 1, k + 2 - NG, 1 - par)
                    ahead = k + 2 < NG or not last
                    if ahead:
                        bias1(*nxt)
                    bias2(t, k, 1)
                    if k >= 2:
                        bias3(t, k - 2)
                    elif not first:
                        bias3(t - 1, NG - 2 + k)
                    if k == 5 and not first:
                        sdf(t - 1)
                    if not last:
                        if k == 0:
                            f_a()
                        if k == 2:
                            f_b()
                        if k == 4:
                            f_c()

            act.wait_ge(s_dve0, 1)
            with act.Fori(0, B) as b:
                t0 = fresh(act, b * T + 1)
                group_norm(b * 2)
                act.wait_ge(s_nb, b * 2 + 1)
                sq_, rs_, ez_, ec_, parts_, sp_ = prep(t0)
                sq_()
                rs_()
                ec_()
                ez_(0)
                parts_(0)
                ez_(1)
                sp_()
                decay(t0, 0, 0)
                copy_c(t0, 0)
                walk(act, b, layer0)
                group_norm(b * 2 + 1)
                act.wait_ge(s_nb, b * 2 + 2)
                t1st = fresh(act, b * T + 1)
                for f in features(t1st, 0):
                    f()
                for k in range(2):
                    bias1(t1st, k, 0)
                walk(act, b, layer1)
                t9 = fresh(act, b * T + T)
                bias3(t9, NG - 2)
                bias3(t9, NG - 1)
                sdf(t9)

        @block.gpsimd
        def _(pool):
            chunk_zero(pool, pool_counts)

            def gate(t, par):
                pool.wait_ge(s_yv, t + 1)
                pool.wait_ge(s_sz, t * 2 + 2)
                nc.gpsimd.tensor_tensor(yo, yo, sz[par], ALU.mult).then_inc(s_gate, 1)

            def times_c(t, n):
                pool.wait_ge(s_Ccp, t * NS + (n + 1))
                pool.wait_ge(s_scan[0], t * NS + (n + 1))
                pool.wait_ge(s_scan[1], t * NS + (n + 1))
                pool.wait_ge(s_sum, t * NS + (n + 1 - CR))
                c = csb[n % CR].rearrange("p (o l) -> p o l", o=1).to_broadcast([P, 2, L])
                nc.gpsimd.tensor_tensor(ch[n % CR], H[:, n % HR, :, :], c, ALU.mult).then_inc(s_ch, 1)

            def layer0(t, pair, i, col, par, first, last):
                for n in range(NS):
                    times_c(t, n)
                    if n == 3 and not first:
                        gate(t - 1, 1 - par)

            def bias1_last(t, k, par):
                if k == 0:
                    pool.wait_ge(s_g, t + 1)
                pool.wait_ge(s_m2, t * (2 * NG) + 2 * (k - 3))
                q = GQ * k + GQ - 2
                features = g[par].rearrange("p (o l) -> p o l", o=1).to_broadcast([P, 2, L])
                quads = ptb[:, q:q + 2].rearrange("p (q o) -> p q o", o=1).to_broadcast([P, 2, L])
                nc.gpsimd.tensor_tensor(t1[k % 4][:, GQ - 2:, :], features, quads, ALU.add).then_inc(s_t1p, 1)

            def leaky3(t, k):
                pool.wait_ge(s_t3, t * NG + (k + 1))
                nc.gpsimd.tensor_tensor(t3[k % 4], t3[k % 4], t3s[k % 2], ALU.add).then_inc(s_l3, 1)

            def layer1(t, pair, i, col, par, first, last):
                for k in range(NG):
                    if k + 2 < NG:
                        bias1_last(t, k + 2, par)
                    elif not last:
                        bias1_last(t + 1, k + 2 - NG, 1 - par)
                    if k >= 2:
                        leaky3(t, k - 2)
                    elif not first:
                        leaky3(t - 1, NG - 2 + k)

            with pool.Fori(0, B) as b:
                walk(pool, b, layer0)
                gate(b * T + T, 1)
                t1st = fresh(pool, b * T + 1)
                bias1_last(t1st, 0, 0)
                bias1_last(t1st, 1, 0)
                walk(pool, b, layer1)
                t9 = fresh(pool, b * T + T)
                leaky3(t9, NG - 2)
                leaky3(t9, NG - 1)

        @block.vector
        def _(dve):
            V = nc.vector
            chunk_zero(dve, dve_counts)
            dve.wait_ge(s_w, W_ALL)
            V.memset(epsc[:, :], EPS).then_inc(s_dve0, 1)
            win = w_x.rearrange("p (o n) -> p o n", o=1).to_broadcast([P, TAPS, 2 * P])
            V.tensor_tensor(w_conv[:, :, :, :].rearrange("p k h n -> p k (h n)"), tapw, win, ALU.mult).then_inc(s_dve0, 1)
            dve.wait_ge(s_act0, 1)
            V.tensor_scalar(a_neg[:, :, :], a_neg[:, :, :], -1.0, None, ALU.mult).then_inc(s_dve0, 1)
            dve.wait_ge(s_pe0, 2)
            V.tensor_copy(gw[:, :], ps[0:32, 0, 0:P]).then_inc(s_dve0, 1)
            V.tensor_tensor(gb[:, :], bm1[:, :], ps[:, 1, 0:1], ALU.add).then_inc(s_dve0, 1)
            V.tensor_scalar(bm3s[:, 0:1], bm3[:, :], SLOPE, None, ALU.mult).then_inc(s_dve0, 1)
            V.tensor_scalar(bm3s[:, 1:2], bm3[:, :], 1 - SLOPE, None, ALU.mult).then_inc(s_dve0, 1)
            dve.wait_ge(s_dve0, 7)
            V.tensor_scalar(ptb[:, :], pts[:, :], m1p[:, :], gb[:, :], ALU.mult, ALU.add).then_inc(s_dve0, 1)
            dve.wait_ge(s_dve0, 8)

            def group_norm(k):
                plain(dve)
                V.bn_aggr(mv[:, :], stats[:, :, :]).then_inc(s_mv, 1)
                dve.wait_ge(s_gm, k + 1)
                dve.wait_ge(s_mv, k + 1)
                V.tensor_tensor(dev[:, :], mv[:, 0:1], pp[:, 0, 0:1], ALU.subtract).then_inc(s_dev, 1)
                dve.wait_ge(s_dev, k + 1)
                V.scalar_tensor_tensor(out=vd[:, :], in0=dev[:, :], scalar=dev[:, :], in1=mv[:, 1:2],
                                       op0=ALU.mult, op1=ALU.add).then_inc(s_vd, 1)
                dve.wait_ge(s_gr, k + 1)
                V.scalar_tensor_tensor(out=gs[:, :], in0=pp[:, 0, 0:1], scalar=-1.0, in1=gr[:, :],
                                       op0=ALU.mult, op1=ALU.mult).then_inc(s_gs, 1)
                dve.wait_ge(s_cs, k + 1)

            def prep(t):
                def normed():
                    dve.wait_ge(s_rs, t + 1)
                    V.scalar_tensor_tensor(out=ln[:, :], in0=pp[:, 0, :], scalar=cs[:, :], in1=ln[:, :],
                                           op0=ALU.add, op1=ALU.mult).then_inc(s_xn, 1)

                def affine(carry):
                    dve.wait_ge(s_cv, t * 2)
                    dve.wait_ge(s_z, t * 2)
                    if carry:
                        V.tensor_copy(xnf[:, 0:TAPS - 1], xnf[:, L:L + TAPS - 1]).then_inc(s_car, 1)
                    else:
                        V.memset(xnf[:, 0:TAPS - 1], 0.0).then_inc(s_car, 1)
                    dve.wait_ge(s_car, t + 1)
                    dve.wait_ge(s_xn, t + 1)
                    V.tensor_scalar(xnf[:, TAPS - 1:], ln[:, :], lnw[:, :], lnb[:, :], ALU.mult, ALU.add).then_inc(s_xnf, 1)

                def limit_z(h):
                    dve.wait_ge(s_z, t * 2 + (h + 1))
                    V.tensor_scalar(exz, qp, SIGMOID_ZERO, None, ALU.max).then_inc(s_kz, 1)

                def silu_z(par, h, start=False):
                    dve.wait_ge(s_rz, t * 2 + (h + 1))
                    if not start:
                        dve.wait_ge(s_gate, t - 1)
                    V.tensor_tensor(sz[par][:, h, :], exz, qp, ALU.mult).then_inc(s_sz, 1)

                def limit_c():
                    dve.wait_ge(s_cv, t * 2 + 2)
                    for h in range(2):
                        m = V.tensor_scalar(ex[:, h, :], pp[:, h, :], cb[:, h:h + 1], SIGMOID_ZERO, ALU.add, ALU.max)
                    m.then_inc(s_kc, 1)

                def silu_c(par):
                    dve.wait_ge(s_rc, t + 1)
                    for h in range(2):
                        m = V.scalar_tensor_tensor(out=u[par][:, h, :], in0=pp[:, h, :], scalar=cb[:, h:h + 1],
                                                   in1=ex[:, h, :], op0=ALU.add, op1=ALU.mult)
                    m.then_inc(s_u, 1)

                def parts(par):
                    dve.wait_ge(s_hi, t + 1)
                    dve.wait_ge(s_xnf, t + 1)
                    dve.wait_ge(s_u, t + 1)
                    V.tensor_tensor(ln[0:96, :], pp[0:96, 0, :], bc[par][:, :], ALU.subtract).then_inc(s_rest, 1)
                    dve.wait_ge(s_rest, t + 1)
                    V.tensor_copy(bc[par][32:64, :], ln[32:64, :]).then_inc(s_mid, 1)
                    V.tensor_copy(mid, ln[64:96, :]).then_inc(s_mid, 1)
                    dve.wait_ge(s_mid, t * 2 + 2)
                    V.tensor_tensor(bc[par][64:96, :], ln[64:96, :], mid, ALU.subtract).then_inc(s_lo, 1)

                def clamp():
                    dve.wait_ge(s_dt, t + 1)
                    dve.wait_ge(s_lo, t + 1)
                    for h in range(2):
                        m = V.tensor_scalar(ex[:, h, :], pp[:, h, :], bdt[:, h:h + 1], SOFTPLUS_LINEAR, ALU.add, ALU.min)
                    m.then_inc(s_tm, 1)

                def steps(par, start=False):
                    dve.wait_ge(s_sp, t + 1)
                    if not start:
                        dve.wait_ge(s_dA[1], (t - 1) * NS)
                    for h in range(2):
                        m = V.scalar_tensor_tensor(out=delta[par][:, h, :], in0=pp[:, h, :], scalar=bdt[:, h:h + 1],
                                                   in1=ex[:, h, :], op0=ALU.add, op1=ALU.max)
                    m.then_inc(s_del, 1)
                    dve.wait_ge(s_del, t + 1)
                    V.tensor_tensor(du[par], delta[par], u[par], ALU.mult).then_inc(s_du, 1)

                return normed, affine, limit_z, silu_z, limit_c, silu_c, parts, clamp, steps

            def times_b(t, n, par):
                dve.wait_ge(s_B, t * NS + (n + 1))
                dve.wait_ge(s_scan[1], t * NS + (n - 1))
                if n == 0:
                    dve.wait_ge(s_du, t + 1)
                bb = B_ps[n % 2].rearrange("p (o l) -> p o l", o=1).to_broadcast([P, 2, L])
                V.tensor_tensor(dbu[n % 2], du[par], bb, ALU.mult).then_inc(s_mulb, 1)

            def keep_last(t, n, first):
                if n == 0 and first:
                    dve.sem_inc(s_last, 1)
                    return
                dve.wait_ge(s_scan[0], t * NS + n)
                dve.wait_ge(s_scan[1], t * NS + n)
                m, k = (n - 4) % NS, (n - 4) % HR
                V.tensor_copy(carried[:, m:m + 4, :], H[:, k:k + 4, :, L - 1]).then_inc(s_last, 1)

            def scan(t, n):
                dve.wait_ge(s_mulb, t * NS + (n + 1))
                dve.wait_ge(s_ch, t * NS + (n + 1 - HR))
                dve.wait_ge(s_last, t * (NS // 4) + n // 4)
                for h in range(2):
                    dve.wait_ge(s_dA[h], t * NS + (n + 1))
                    V.tensor_tensor_scan(H[:, n % HR, h, :], dA[n % 2][:, h, :], dbu[n % 2][:, h, :],
                                         carried[:, n, h:h + 1], ALU.mult, ALU.add).then_inc(s_scan[h], 1)

            def y_out(t, par):
                dve.wait_ge(s_sum, t * NS + NS)
                dve.wait_ge(s_o, t)
                for h in range(2):
                    m = V.scalar_tensor_tensor(out=yo[:, h, :], in0=u[par][:, h, :], scalar=dsk[:, h:h + 1],
                                               in1=y_ps[:, h, :], op0=ALU.mult, op1=ALU.add)
                m.then_inc(s_yv, 1)

            def residual(t, col, i):
                xc = X[:, bass.ds(col, L)]
                st = stats[:, bass.ds(i, 1), :].rearrange("p o s -> p (o s)")
                dve.wait_ge(s_o, t + 1)
                V.tensor_tensor(xc, xc, qp, ALU.add).then_inc(s_res, 1)
                dve.wait_ge(s_res, t + 1)
                plain(dve)
                V.bn_stats(st, xc).then_inc(s_st1, 1)

            def layer0(t, pair, i, col, par, first, last):
                n_, a_, lz_, sz_, lc_, sc_, pa_, cl_, st_ = prep(t + 1)
                for n in range(NS):
                    if n + 1 < NS:
                        times_b(t, n + 1, par)
                    elif not last:
                        times_b(t + 1, 0, 1 - par)
                    if n % 4 == 0:
                        keep_last(t, n, first)
                    scan(t, n)
                    if n == 3 and not first:
                        y_out(t - 1, 1 - par)
                    if n == 7 and not first:
                        residual(t - 1, col - L, i - 1)
                    if not last:
                        if n == 2:
                            n_()
                            a_(True)
                        if n == 7:
                            lc_()
                        if n == 9:
                            sc_(1 - par)
                        if n in (8, 11):
                            lz_((n - 8) // 3)
                        if n in (10, 13):
                            sz_(1 - par, (n - 10) // 3)
                        if n == 11:
                            pa_(1 - par)
                        if n == 12:
                            cl_()
                        if n == 14:
                            st_(1 - par)

            def leaky(ap, s):
                V.scalar_tensor_tensor(out=ap, in0=ap, scalar=SLOPE, in1=ap, op0=ALU.mult, op1=ALU.max).then_inc(s, 1)

            def features(t):
                def first_layer():
                    dve.wait_ge(s_f1a, t + 1)
                    leaky(f1, s_f1l)

                def second_layer():
                    dve.wait_ge(s_f2a, t + 1)
                    leaky(f2, s_f2l)

                return first_layer, second_layer

            def flat(ap):
                return ap.rearrange("p k l -> p (k l)")

            def leaky1(t, k):
                dve.wait_ge(s_t1, t * NG + (k + 1))
                dve.wait_ge(s_t1p, t * NG + (k + 1))
                leaky(flat(t1[k % 4]), s_l1)

            def leaky2(t, k):
                dve.wait_ge(s_t2, t * (2 * NG) + (2 * k + 2))
                leaky(flat(t2[k % 4]), s_l2)

            def limit(t):
                dve.wait_ge(s_m4, t * (NG // 2) + NG // 2)
                dve.wait_ge(s_ob, t)
                V.tensor_scalar(sg, m4_ps, bm4[:, :], SIGMOID_ZERO, ALU.add, ALU.max).then_inc(s_lim, 1)

            def sdf(t, col, par):
                dve.wait_ge(s_sg, t + 1)
                V.tensor_tensor(ob[par], sg, X[:, bass.ds(col, L)], ALU.add).then_inc(s_ob, 1)

            def layer1(t, pair, i, col, par, first, last):
                f_a, f_b = features(t + 1)
                for k in range(NG):
                    if k + 1 < NG:
                        leaky1(t, k + 1)
                    elif not last:
                        leaky1(t + 1, 0)
                    leaky2(t, k)
                    if k == 4 and not first:
                        limit(t - 1)
                    if k == 6 and not first:
                        if par == 1:
                            dve.wait_ge(s_out[0], pair * 16)
                        else:
                            dve.wait_ge(s_out[1], (pair - 1) * 16)
                        sdf(t - 1, col - L, 1 - par)
                    if not last:
                        if k == 1:
                            f_a()
                        if k == 3:
                            f_b()

            with dve.Fori(0, B) as b:
                t0 = fresh(dve, b * T + 1)
                dve.wait_ge(s_x, (b + 1) * (16 * XPARTS))
                for par in range(2):
                    dve.wait_ge(s_out[par], b * (16 * PAIRS) + 16)
                plain(dve)
                with dve.Fori(0, T) as i:
                    V.bn_stats(stats[:, bass.ds(i, 1), :].rearrange("p o s -> p (o s)"), X[:, bass.ds(i * L, L)]).then_inc(s_st, 1)
                dve.wait_ge(s_st, (b + 1) * T)
                group_norm(b * 2)
                V.tensor_scalar(cen_r[:, :], cen[:, :], gr[:, :], None, ALU.mult).then_inc(s_agg, 1)
                V.tensor_copy(cs[:, :], ps[:, 7, 0:1]).then_inc(s_h0, 1)
                V.memset(carried[:, :, :], 0.0).then_inc(s_h0, 1)
                dve.wait_ge(s_agg, b * 2 + 1)
                dve.wait_ge(s_h0, (b + 1) * 2)
                dve.sem_inc(s_nb, 1)
                n_, a_, lz_, sz_, lc_, sc_, pa_, cl_, st_ = prep(t0)
                n_()
                a_(False)
                lc_()
                lz_(0)
                sc_(0)
                sz_(0, 0, True)
                pa_(0)
                lz_(1)
                sz_(0, 1, True)
                cl_()
                st_(0, True)
                times_b(t0, 0, 0)

                walk(dve, b, layer0)
                t9 = fresh(dve, b * T + T)
                y_out(t9, 1)
                residual(t9, (T - 1) * L, T - 1)
                dve.wait_ge(s_st1, t9 + 1)

                group_norm(b * 2 + 1)
                V.tensor_scalar(s1r[:, :], s1[:, :], gr[:, :], None, ALU.mult).then_inc(s_agg, 1)
                V.tensor_tensor(b1r[:, :], bs1[:, :], ps[0:64, 7, 0:1], ALU.add).then_inc(s_nw, 1)
                dve.wait_ge(s_agg, b * 2 + 2)
                dve.wait_ge(s_nw, b + 1)
                dve.sem_inc(s_nb, 1)
                t1st = fresh(dve, b * T + 1)
                for f in features(t1st):
                    f()
                leaky1(t1st, 0)
                walk(dve, b, layer1)
                t9 = fresh(dve, b * T + T)
                limit(t9)
                dve.wait_ge(s_out[1], (b * PAIRS + PAIRS) * 16)
                sdf(t9, (T - 1) * L, 1)


def kernel(**inputs):
    import numpy as np
    import concourse.bacc as bacc
    import ml_dtypes
    from concourse import mybir as mb
    from concourse.bass_utils import run_bass_kernel_spmd as run

    q = {k: np.ascontiguousarray(v) for k, v in inputs.items()}
    B, C, Hh, Ww = q["x"].shape
    f = np.float32

    def halves(a):
        return np.ascontiguousarray(a.reshape(2, P, -1).transpose(1, 0, 2))

    def col(a):
        return np.ascontiguousarray(a.reshape(-1, 1))

    xp_t = q["L0_conv_W_xproj"].T
    xp_t = np.concatenate([xp_t[:, DTR:]] * 3 + [xp_t[:, :DTR]], axis=1)
    mw1, mw2, mw3, mw4 = (q[f"L1_conv_mw{i}"] for i in (1, 2, 3, 4))
    mw2_bd = np.zeros((P, P), f)
    mw3_bd = np.zeros((P, 64), f)
    mw4_bd = np.zeros((P, 4, 32), f)
    for j in range(4):
        mw2_bd[32 * j:32 * j + 32, 32 * j:32 * j + 32] = mw2.T
        mw3_bd[32 * j:32 * j + 32, 16 * j:16 * j + 16] = mw3.T
    for k in range(4):
        for j in range(8):
            mw4_bd[16 * j:16 * j + 16, k, 8 * k + j] = mw4[0]
    eye = np.eye(P, dtype=f)
    c = np.arange(P)
    gm = ((c[:, None] // 4) == (c[None, :] // 4)).astype(f) / 4
    om = np.full((P, 1), 1.0 / P, f)
    pick = np.zeros((96, 2 * NS), ml_dtypes.bfloat16)
    for k in range(96):
        pick[k, k % 32] = 1
    lin = np.linspace(-1.0, 1.0, P, dtype=f)
    points = np.zeros((P, NG * GQ), f)
    for quad in range(NG * GQ):
        s, e = quad // 2, quad % 2
        for j in range(4):
            points[32 * j:32 * j + 32, quad] = lin[32 * (s % 4) + 8 * (s // 4) + 4 * e + j]

    arrays = dict(
        x=q["x"].reshape(B, C, Hh * Ww),
        w_in_t=np.ascontiguousarray(q["L0_conv_W_in"].T),
        conv_w_t=np.ascontiguousarray(q["L0_conv_conv_w"].T),
        conv_b=halves(q["L0_conv_conv_b"].reshape(-1, 1))[:, :, 0],
        ln_w=col(q["L0_conv_ln_w"]), ln_b=col(q["L0_conv_ln_b"]),
        w_xproj_t=halves(xp_t),
        w_dt_t=np.ascontiguousarray(q["L0_conv_W_dt"].T.reshape(DTR, 2, P)),
        b_dt=halves(q["L0_conv_b_dt"].reshape(-1, 1))[:, :, 0],
        a_log=halves(q["L0_conv_A_log"]),
        d_skip=halves(q["L0_conv_D"].reshape(-1, 1))[:, :, 0],
        w_out_t=halves(q["L0_conv_W_out"].T),
        sw1_t=q["L1_conv_sw1"].T, sb1=col(q["L1_conv_sb1"]), sw2_t=q["L1_conv_sw2"].T, sb2=col(q["L1_conv_sb2"]),
        sw3=q["L1_conv_sw3"], sb3=col(q["L1_conv_sb3"]),
        mw1_t=np.tile(mw1[:, :16].T, (1, 4)), mw1_pt=col(np.tile(mw1[:, 16], 4)), mb1=col(np.tile(q["L1_conv_mb1"], 4)),
        mw2_bd=mw2_bd, mb2=col(np.tile(q["L1_conv_mb2"], 4)), mw3_bd=mw3_bd, mb3=col(np.tile(q["L1_conv_mb3"], 8)),
        mw4_bd=mw4_bd, mb4=col(np.tile(q["L1_conv_mb4"], P)),
        center=eye - 1.0 / f(P), group_mean=gm, ones_mean=om, ident=eye, pick=pick, points=points,
    )
    nc = bacc.Bacc("TRN2", target_bir_lowering=False, num_devices=1)
    feed, args = {}, []
    for name, a in arrays.items():
        a = np.ascontiguousarray(a)
        feed["in_" + name] = a
        args.append(nc.dram_tensor("in_" + name, a.shape, mb.dt.from_np(a.dtype), kind="ExternalInput").ap())
    out = nc.dram_tensor("out", (B, C, Hh * Ww), mb.dt.float32, kind="ExternalOutput").ap()
    mamba_sdf_kernel(nc, *args, out)
    r = run(nc, [feed], core_ids=[0])
    return r.results[0]["out"].reshape(B, C, Hh, Ww)
```

```python
from contextlib import ExitStack

import concourse.bass as bass
from concourse import mybir

F32 = mybir.dt.float32
BF16 = mybir.dt.bfloat16
ALU = mybir.AluOpType
ACT = mybir.ActivationFunctionType

P = 128
L = 512
NS = 16
TAPS = 4
DTR = 8
HR = 8
CR = 4
PAIRED = (11,)
SUMS_BEFORE = {0: (14,), 1: (15,)}
SUMS = {3: (0,), 4: (1,), 5: (2,), 6: (3,), 7: (4,), 8: (5,), 9: (6,), 10: (7,), 11: (8,), 12: (9,), 13: (11,), 14: (12,), 15: (13,)}
GQ = 4
NG = 8
SLOPE = 0.01
SIGMOID_ZERO = -44.0
EPS = 1e-5


def mamba_sdf_kernel(nc, x, w_in_t, conv_w_t, conv_b, ln_w, ln_b, w_xproj_t, w_dt_t, b_dt, a_log,
                     d_skip, w_out_t, sw1_t, sb1, sw2_t, sb2, sw3, sb3, mw1_t, mw1_pt, mb1, mw2_bd, mb2,
                     mw3_bd, mb3, mw4_bd, mb4, center, group_mean, ones_mean, ident, pick, points, out):
    B, _, N = x.shape
    T = N // L
    PAIRS = T // 2

    with ExitStack() as ctx:
        def sb(name, shape, dt=F32):
            return ctx.enter_context(nc.sbuf_tensor(name, shape, dt))

        def sem(name):
            return ctx.enter_context(nc.semaphore(name))

        w_z = sb("w_z", [P, 2 * P])
        w_conv = sb("w_conv", [P, TAPS, 2, P])
        cb = sb("cb", [P, 2])
        lnw = sb("lnw", [P, 1])
        lnb = sb("lnb", [P, 1])
        w_xp = sb("w_xp", [P, 2, 104])
        w_dt = sb("w_dt", [104, 2, P])
        bdt = sb("bdt", [P, 2])
        a_neg = sb("a_neg", [P, 2, NS])
        dsk = sb("dsk", [P, 2])
        w_out = sb("w_out", [P, 2, P])
        cen = sb("cen", [P, P])
        gmean = sb("gmean", [P, P])
        omean = sb("omean", [P, 1])
        idn = sb("idn", [P, P])
        pk = sb("pk", [96, 2 * NS], BF16)
        s1 = sb("s1", [P, 64])
        bs1 = sb("bs1", [64, 1])
        s2 = sb("s2", [64, 32])
        bs2 = sb("bs2", [32, 1])
        s3 = sb("s3", [16, 32])
        bs3 = sb("bs3", [16, 1])
        m1 = sb("m1", [16, P])
        m1p = sb("m1p", [P, 1])
        bm1 = sb("bm1", [P, 1])
        m2 = sb("m2", [P, P])
        bm2 = sb("bm2", [P, 1])
        m3 = sb("m3", [P, 64])
        bm3 = sb("bm3", [P, 1])
        bm3s = sb("bm3s", [P, 2])
        m4 = sb("m4", [P, 4, 32])
        bm4 = sb("bm4", [P, 1])
        pts = sb("pts", [P, NG * GQ])
        ptb = sb("ptb", [P, NG * GQ])
        gw = sb("gw", [32, P])
        gb = sb("gb", [P, 1])
        epsc = sb("epsc", [P, 1])

        X = sb("X", [P, N])
        stats = sb("stats", [P, T, 6])
        mv = sb("mv", [P, 2])
        dev = sb("dev", [P, 1])
        vd = sb("vd", [P, 1])
        lnv = sb("lnv", [P, 1])
        gr = sb("gr", [P, 1])
        gs = sb("gs", [P, 1])
        cen_r = sb("cen_r", [P, P])
        cs = sb("cs", [P, 1])
        s1r = sb("s1r", [P, 64])
        b1r = sb("b1r", [64, 1])

        arena = sb("arena", [P, 58 * L])

        def over(k, n):
            return arena[:, k * L:(k + n) * L]

        def halves(k):
            return over(k, 2).rearrange("p (h l) -> p h l", h=2)

        H = over(0, 2 * HR).rearrange("p (n h l) -> p n h l", n=HR, h=2)
        ch = [halves(16 + 2 * i) for i in range(CR)]
        csb = [over(24 + i, 1) for i in range(CR)]
        dbu = [halves(28 + 2 * i) for i in range(4)]
        dA = [halves(36 + 2 * i) for i in range(2)]
        delta = [halves(40 + 2 * i) for i in range(2)]
        du = halves(44)
        u = [halves(46 + 2 * i) for i in range(2)]
        sz = [halves(50 + 2 * i) for i in range(2)]
        yo = halves(54)
        exz = halves(56)
        carried = sb("carried", [P, NS, 2])
        bc = [sb(f"bc{i}", [96, L], BF16) for i in range(2)]
        ln = sb("ln", [P, L])
        dts = ln
        xnf = sb("xnf", [P, TAPS - 1 + L])
        ex = sb("ex", [P, 2, L])
        mid = yo[64:96, 0, 0:L // 2].bitcast(BF16)
        w_x = csb[0][:, 0:2 * P]
        tapw = over(16, 2).rearrange("p (k n) -> p k n", n=2 * P)

        t1 = [over(4 * i, 4).rearrange("p (k l) -> p k l", k=GQ) for i in range(4)]
        t2 = [over(16 + 4 * i, 4).rearrange("p (k l) -> p k l", k=GQ) for i in range(4)]
        t3 = [over(32 + 2 * i, 2).rearrange("p (k l) -> p k l", k=2) for i in range(4)]
        t3s = [over(47 + 2 * i, 2).rearrange("p (k l) -> p k l", k=2) for i in range(2)]
        g = [over(40 + i, 1) for i in range(2)]
        f1 = over(42, 1)[0:64]
        f2 = over(43, 1)[0:32]
        sg = over(44, 1)
        ob = [over(45 + i, 1) for i in range(2)]

        ps = ctx.enter_context(nc.psum_tensor("ps", [P, 8, L], F32))
        y_ps, pp = ps[:, 0:2, :], ps[:, 2:4, :]
        B_ps, C_ps, qp = [ps[:, 4, :], ps[:, 5, :]], ps[:, 6, :], ps[:, 7, :]
        m2_ps = [ps[:, 0:2, :], ps[:, 4:6, :]]
        m3_ps = ps[:, 6:8, :]
        m4_ps, f_ps = ps[:, 2, :], ps[:, 3, :]

        s_w = sem("s_weights_loaded")
        s_act0, s_dve0, s_pe0 = sem("s_act_setup"), sem("s_dve_setup"), sem("s_pe_setup")
        s_x0 = [sem(f"s_x_first{i}") for i in range(4)]
        s_x = [sem("s_x_loaded0"), sem("s_x_loaded1")]
        s_carry = sem("s_carry_wait")
        s_mv, s_gm, s_vd, s_gv = sem("s_mean_var"), sem("s_group_mean"), sem("s_group_dev"), sem("s_group_var")
        s_dev, s_lnv, s_gr, s_gs = sem("s_dev"), sem("s_log_var"), sem("s_group_rstd"), sem("s_group_shift")
        s_nw, s_cs, s_nb = sem("s_norm_weights"), sem("s_shift_product"), sem("s_norm_bias")
        s_st, s_agg, s_h0 = sem("s_stats"), sem("s_aggregated"), sem("s_state_cleared")
        s_last, s_pair = sem("s_last_copied"), sem("s_pair_added")
        s_cen, s_sq, s_var, s_lv, s_rs = sem("s_centered"), sem("s_squared"), sem("s_variance"), sem("s_logvar"), sem("s_rstd")
        s_xn, s_car, s_xnf = sem("s_normed"), sem("s_carried"), sem("s_affine")
        s_zc, s_cc = sem("s_z_copied"), sem("s_conv_biased")
        s_z, s_kz, s_ez, s_lz, s_rz, s_sz = sem("s_z"), sem("s_limited_z"), sem("s_exp_z"), sem("s_log_z"), sem("s_sigmoid_z"), sem("s_silu_z")
        s_cv, s_kc, s_ec, s_lc, s_rc, s_u = sem("s_conv"), sem("s_limited_c"), sem("s_exp_c"), sem("s_log_c"), sem("s_sigmoid_c"), sem("s_u")
        s_xd, s_hi, s_dts, s_rest, s_mid, s_lo = sem("s_xdbl"), sem("s_bc_high"), sem("s_dt_copied"), sem("s_bc_rest"), sem("s_bc_mid"), sem("s_bc_low")
        s_dt, s_ab, s_rl, s_ed, s_sp, s_del, s_du = sem("s_dt"), sem("s_abs_dt"), sem("s_relu_dt"), sem("s_exp_dt"), sem("s_log_dt"), sem("s_delta"), sem("s_delta_u")
        s_B, s_C, s_mulb, s_dA0, s_dA1 = sem("s_B_spread"), sem("s_C_spread"), sem("s_dBu"), sem("s_decay0"), sem("s_decay1")
        s_dA = [s_dA0, s_dA1]
        s_scan = [sem("s_scan0"), sem("s_scan1")]
        s_Ccp, s_ch, s_sum = sem("s_C_copied"), sem("s_Ch"), sem("s_summed")
        s_yv, s_gate, s_o, s_res, s_st1 = sem("s_y_out"), sem("s_gated"), sem("s_projected"), sem("s_residual"), sem("s_stats1")
        s_f1, s_f1a, s_f1l = sem("s_f1"), sem("s_f1_biased"), sem("s_f1_relu")
        s_f2, s_f2a, s_f2l = sem("s_f2"), sem("s_f2_biased"), sem("s_f2_relu")
        s_gp, s_g = sem("s_g_product"), sem("s_g")
        s_t1, s_t1p, s_l1, s_m2 = sem("s_h1_biased"), sem("s_h1_biased_last"), sem("s_h1"), sem("s_mm2")
        s_t2, s_l2, s_m3 = sem("s_h2_biased"), sem("s_h2"), sem("s_mm3")
        s_t3, s_l3, s_m4 = sem("s_h3_biased"), sem("s_h3"), sem("s_mm4")
        s_lim = sem("s_sdf_limited")
        s_e, s_le, s_sg, s_ob, s_out = sem("s_sdf_exp"), sem("s_sdf_log"), sem("s_sdf"), sem("s_out_ready"), [sem("s_out_stored0"), sem("s_out_stored1")]

        pe_counts = {s_cen: 1, s_var: 1, s_z: 2, s_cv: 2, s_xd: 1, s_dt: 1, s_B: NS, s_C: NS, s_sum: NS, s_o: 1,
                     s_f1: 1, s_f2: 1, s_gp: 1, s_m2: 2 * NG, s_m3: NG, s_m4: NG // 2}
        act_counts = {s_mid: 2, s_sq: 1, s_lv: 1, s_rs: 1, s_zc: 2, s_cc: 2, s_ab: 1, s_rl: 1, s_ez: 1, s_lz: 1, s_rz: 1, s_ec: 1, s_lc: 1, s_rc: 1, s_hi: 1, s_dts: 1,
                      s_ed: 1, s_sp: 1, s_dA0: NS, s_dA1: NS, s_Ccp: NS, s_f1a: 1, s_f2a: 1, s_g: 1,
                      s_t1: NG, s_t2: 2 * NG, s_t3: NG, s_e: 1, s_le: 1, s_sg: 1}
        pool_counts = {s_pair: len(PAIRED), s_u: 1, s_sz: 1, s_ch: NS, s_gate: 1, s_t1p: NG, s_l3: NG}
        dve_counts = {s_xn: 1, s_car: 1, s_xnf: 1, s_kz: 1, s_last: NS // 4, s_kc: 1, s_rest: 1, s_lo: 1,
                      s_del: 1, s_du: 1, s_mulb: NS, s_scan[0]: NS, s_scan[1]: NS, s_yv: 1, s_res: 1, s_st1: 1,
                      s_f1l: 1, s_f2l: 1, s_l1: NG, s_l2: NG, s_lim: 1, s_ob: 1}

        def chunk_zero(eng, counts):
            for s, n in counts.items():
                eng.sem_inc(s, n)

        loads = [
            (w_x, w_in_t[:, 0:2 * P]), (w_z[:], w_in_t[:, 2 * P:4 * P]), (tapw, conv_w_t.partition_broadcast(P)), (cb[:], conv_b), (lnw[:], ln_w), (lnb[:], ln_b),
            (w_xp[:], w_xproj_t), (w_dt[96:104], w_dt_t), (bdt[:], b_dt), (a_neg[:], a_log), (dsk[:], d_skip),
            (w_out[:], w_out_t), (cen[:], center), (gmean[:], group_mean), (omean[:], ones_mean), (idn[:], ident),
            (pk[:], pick), (s1[:], sw1_t), (bs1[:], sb1), (s2[:], sw2_t), (bs2[:], sb2), (s3[:], sw3), (bs3[:], sb3),
            (m1[:], mw1_t), (m1p[:], mw1_pt), (bm1[:], mb1), (m2[:], mw2_bd), (bm2[:], mb2), (m3[:], mw3_bd),
            (bm3[:], mb3), (m4[:], mw4_bd), (bm4[:], mb4), (pts[:], points),
        ]
        W_ALL = 16 * len(loads)

        def fresh(eng, value):
            if isinstance(value, int):
                return value
            return eng.snap(eng.to_reg(value))

        def plain(eng):
            eng.sem_inc(s_carry, 1)

        def walk(eng, b, chunk):
            for par in range(2):
                chunk(fresh(eng, b * T + (1 + par)), fresh(eng, b * PAIRS + 1), par, par * L, par, par == 0, 2)
            with eng.Fori(1, PAIRS - 1) as j:
                for par in range(2):
                    chunk(fresh(eng, b * T + j * 2 + (1 + par)), fresh(eng, b * PAIRS + j + 1), j * 2 + par,
                          fresh(eng, j * (2 * L) + par * L), par, False, 2)
            for par in range(2):
                i = T - 2 + par
                chunk(fresh(eng, b * T + (i + 1)), fresh(eng, b * PAIRS + PAIRS), i, i * L, par, False, 1 - par)

        block = ctx.enter_context(nc.Block())

        @block.sync
        def _(sp):
            chunk_zero(sp, {s_out[0]: 16, s_out[1]: 16})
            for k in range(4):
                w = N // 4
                sp.dma_start(X[:, k * w:(k + 1) * w], x[0, :, k * w:(k + 1) * w]).then_inc(s_x0[k], 16)

            def image(b, more):
                def chunk(t, pair, i, col, par, first, ahead):
                    sp.wait_ge(s_ob, t + 1)
                    sp.dma_start(out[b, :, bass.ds(col, L)], ob[par]).then_inc(s_out[par], 16)
                    if more:
                        sp.dma_start(X[:, bass.ds(col, L)], x[b + 1, :, bass.ds(col, L)]).then_inc(s_x[par], 16)
                    else:
                        sp.sem_inc(s_x[par], 16)

                walk(sp, b, chunk)

            with sp.Fori(0, B - 1) as b:
                image(b, True)
            image(B - 1, False)
            for par in range(2):
                sp.wait_ge(s_out[par], 16 * (B * PAIRS + 1))

        @block.tensor
        def _(pe):
            mm = nc.tensor.matmul
            chunk_zero(pe, pe_counts)

            pe.wait_ge(s_w, W_ALL)
            mm(ps[0:32, 0, 0:P], s3[:, :], m1[:, :], start=True, stop=True).then_inc(s_pe0, 1)
            mm(ps[:, 1, 0:1], m1[:, :], bs3[:, :], start=True, stop=True).then_inc(s_pe0, 1)

            def group_norm(k, weights, width):
                pe.wait_ge(s_mv, k + 1)
                mm(pp[:, 0, 0:1], gmean[:, :], mv[:, 0:1], start=True, stop=True).then_inc(s_gm, 1)
                pe.wait_ge(s_vd, k + 1)
                mm(pp[:, 1, 0:1], gmean[:, :], vd[:, :], start=True, stop=True).then_inc(s_gv, 1)
                pe.wait_ge(s_gs, k + 1)
                mm(ps[0:width, 7, 0:1], weights, gs[:, :], start=True, stop=True).then_inc(s_cs, 1)

            def prep(t, col):
                def center_it():
                    pe.wait_ge(s_rl, t)
                    mm(pp[:, 0, :], cen_r[:, :], X[:, bass.ds(col, L)], start=True, stop=True).then_inc(s_cen, 1)

                def variance():
                    pe.wait_ge(s_sq, t + 1)
                    mm(pp[:, 1, :], omean[:, :].to_broadcast([P, P]), ln[:, :], start=True, stop=True).then_inc(s_var, 1)

                def z(h, start=False):
                    pe.wait_ge(s_xnf, t + 1)
                    if not start:
                        pe.wait_ge(s_res, t - 1)
                    pe.wait_ge(s_zc, t * 2 + h)
                    mm(qp, w_z[:, h * P:(h + 1) * P], xnf[:, TAPS - 1:], start=True, stop=True).then_inc(s_z, 1)

                def conv(h, a):
                    if h == 0 and a == 0:
                        pe.wait_ge(s_xnf, t + 1)
                        pe.wait_ge(s_lv, t + 1)
                    for k in range(a, a + 2):
                        m = mm(pp[:, h, :], w_conv[:, k, h, :], xnf[:, k:k + L], start=k == 0, stop=k == TAPS - 1)
                    if a == 2:
                        m.then_inc(s_cv, 1)

                def xdbl():
                    pe.wait_ge(s_u, t + 1)
                    for h in range(2):
                        m = mm(pp[0:104, 0, :], w_xp[:, h, :], u_of(t)[:, h, :], start=h == 0, stop=h == 1)
                    m.then_inc(s_xd, 1)

                def step_size():
                    pe.wait_ge(s_dts, t + 1)
                    pe.wait_ge(s_rest, t + 1)
                    for h in range(2):
                        m = mm(pp[:, h, :], w_dt[96:104, h, :], dts[96:104, :], start=True, stop=True)
                    m.then_inc(s_dt, 1)

                return center_it, variance, z, conv, xdbl, step_size

            par_now = [0]

            def u_of(t):
                return u[par_now[0]]

            def spread_b(t, n, par):
                if n == 0:
                    pe.wait_ge(s_lo, t + 1)
                pe.wait_ge(s_mulb, t * NS + (n - 1))
                mm(B_ps[n % 2], pk[:, n:n + 1].to_broadcast([96, P]), bc[par][:, :], start=True, stop=True).then_inc(s_B, 1)

            def spread_c(t, n, par):
                pe.wait_ge(s_Ccp, t * NS + n)
                mm(C_ps, pk[:, NS + n:NS + n + 1].to_broadcast([96, P]), bc[par][:, :], start=True, stop=True).then_inc(s_C, 1)

            def next_c(t, n, par, ahead):
                if n + 1 < NS:
                    spread_c(t, n + 1, par)
                elif ahead:
                    spread_c(t + 1, 0, 1 - par)

            def add_state(t, n):
                if n == 0:
                    pe.wait_ge(s_yv, t)
                if n in PAIRED:
                    pe.wait_ge(s_pair, t * len(PAIRED) + (PAIRED.index(n) + 1))
                else:
                    pe.wait_ge(s_ch, t * NS + (n + 1))
                for h in range(2):
                    m = mm(y_ps[:, h, :], idn[:, :], ch[n % CR][:, h, :], start=n == 0, stop=n == NS - 1)
                m.then_inc(s_sum, 2 if n in PAIRED else 1)

            def project_out(t, z_ahead):
                pe.wait_ge(s_gate, t + 1)
                pe.wait_ge(s_zc, t * 2 + (4 if z_ahead else 2))
                for h in range(2):
                    m = mm(qp, w_out[:, h, :], yo[:, h, :], start=h == 0, stop=h == 1)
                m.then_inc(s_o, 1)

            def layer0(t, pair, i, col, par, first, ahead):
                par_now[0] = 1 - par
                if ahead:
                    cen_, var_, z_, conv_, xd_, dt_ = prep(t + 1, col + L)
                if ahead == 2:
                    next_cen, next_var = prep(t + 2, col + 2 * L)[:2]
                for n in range(NS):
                    if n + 2 < NS:
                        spread_b(t, n + 2, par)
                    elif ahead:
                        spread_b(t + 1, n + 2 - NS, 1 - par)
                    if ahead and n == 11:
                        dt_()
                    if ahead and 2 <= n <= 4:
                        conv_((n - 1) // 2, 2 * ((n - 1) % 2))
                    if 2 <= n <= 5:
                        next_c(t, n, par, ahead)
                    if not first:
                        for k in SUMS_BEFORE.get(n, ()):
                            add_state(t - 1, k)
                    for k in SUMS.get(n, ()):
                        add_state(t, k)
                    if n == 1 and ahead:
                        conv_(0, 0)
                    if not 2 <= n <= 5:
                        next_c(t, n, par, ahead)
                    if n == 6 and not first:
                        project_out(t - 1, True)
                    if ahead:
                        if n == 9:
                            xd_()
                        if n in (10, 13):
                            z_((n - 10) // 3)
                    if ahead == 2:
                        if n == NS - 2:
                            next_cen()
                        if n == NS - 1:
                            next_var()

            def layer0_start(t):
                par_now[0] = 0
                cen_, var_, z_, conv_, xd_, dt_ = prep(t, 0)
                cen_()
                var_()
                for h in range(2):
                    for a in (0, 2):
                        conv_(h, a)
                z_(0, True)
                xd_()
                z_(1, True)
                dt_()
                spread_b(t, 0, 0)
                spread_b(t, 1, 0)
                spread_c(t, 0, 0)
                for f in prep(t + 1, L)[:2]:
                    f()

            def layer0_end(t):
                for n in sum(SUMS_BEFORE.values(), ()):
                    add_state(t, n)
                project_out(t, False)

            def features(t, col, par):
                def first_layer():
                    pe.wait_ge(s_g, t)
                    mm(f_ps[0:64], s1r[:, :], X[:, bass.ds(col, L)], start=True, stop=True).then_inc(s_f1, 1)

                def second_layer():
                    pe.wait_ge(s_f1l, t + 1)
                    plain(pe)
                    mm(f_ps[0:32], s2[:, :], f1, start=True, stop=True).then_inc(s_f2, 1)

                def third_layer():
                    pe.wait_ge(s_f2l, t + 1)
                    mm(f_ps, gw[:, :], f2, start=True, stop=True).then_inc(s_gp, 1)

                return first_layer, second_layer, third_layer

            def mm2(t, k):
                pe.wait_ge(s_l1, t * NG + (k + 1))
                for half in range(2):
                    pe.wait_ge(s_t2, t * (2 * NG) + (2 * k + half - 1))
                    for j in range(2):
                        q = 2 * half + j
                        m = mm(m2_ps[half][:, j, :], m2[:, :], t1[k % 4][:, q, :], start=True, stop=True)
                    m.then_inc(s_m2, 1)

            def mm3(t, k):
                pe.wait_ge(s_l2, t * NG + (k + 1))
                pe.wait_ge(s_t3, t * NG + k)
                for s in range(2):
                    for e in range(2):
                        m = mm(m3_ps[64 * e:64 * e + 64, s, :], m3[:, :], t2[k % 4][:, 2 * s + e, :],
                               start=True, stop=True)
                m.then_inc(s_m3, 1)

            def mm4(t, k):
                pe.wait_ge(s_l3, t * NG + (k + 1))
                if k == 1:
                    pe.wait_ge(s_lim, t)
                for quadrant in range(4):
                    m = mm(m4_ps[32 * quadrant:32 * quadrant + 32, :], m4[:, k // 2, :],
                           t3[(k - 1 + quadrant // 2) % 4][:, quadrant % 2, :], start=k == 1, stop=k == NG - 1)
                m.then_inc(s_m4, 1)

            def layer1(t, pair, i, col, par, first, ahead):
                f_a, f_b, f_c = features(t + 1, col + L, 1 - par)
                for k in range(NG):
                    mm2(t, k)
                    if k >= 2:
                        mm3(t, k - 2)
                    elif not first:
                        mm3(t - 1, NG - 2 + k)
                    if k in (5, 7):
                        mm4(t, k - 4)
                    if k in (1, 3) and not first:
                        mm4(t - 1, NG - 4 + k)
                    if ahead:
                        if k == 0:
                            f_a()
                        if k == 2:
                            f_b()
                        if k == 4:
                            f_c()

            with pe.Fori(0, B) as b:
                t0 = fresh(pe, b * T + 1)
                pe.wait_ge(s_w, W_ALL)
                group_norm(b * 2, cen[:, :], P)
                pe.wait_ge(s_nb, b * 2 + 1)
                layer0_start(t0)
                walk(pe, b, layer0)
                layer0_end(fresh(pe, b * T + T))
                group_norm(b * 2 + 1, s1[:, :], 64)
                pe.wait_ge(s_nb, b * 2 + 2)
                plain(pe)
                for f in features(fresh(pe, b * T + 1), 0, 0):
                    f()
                walk(pe, b, layer1)
                t9 = fresh(pe, b * T + T)
                mm3(t9, NG - 2)
                mm3(t9, NG - 1)
                mm4(t9, NG - 3)
                mm4(t9, NG - 1)

        @block.scalar
        def _(act):
            A = nc.scalar.activation
            chunk_zero(act, act_counts)
            for dst, src in loads:
                act.dma_start(dst, src).then_inc(s_w, 16)
            nc.scalar.preload_act_table_set("natural_log_exp_and_others")
            act.wait_ge(s_w, W_ALL)
            A(a_neg[:, :, :], a_neg[:, :, :], ACT.Exp).then_inc(s_act0, 1)

            def group_norm(k):
                act.wait_ge(s_gv, k + 1)
                A(lnv[:, :], pp[:, 1, 0:1], ACT.Ln, bias=epsc[:, :]).then_inc(s_lnv, 1)
                act.wait_ge(s_lnv, k + 1)
                A(gr[:, :], lnv[:, :], ACT.Exp, scale=-0.5).then_inc(s_gr, 1)

            def prep(t, start=False):
                def square():
                    act.wait_ge(s_cen, t + 1)
                    act.wait_ge(s_lo, t)
                    act.wait_ge(s_dt, t)
                    A(ln[:, :], pp[:, 0, :], ACT.Square, bias=cs[:, :]).then_inc(s_sq, 1)

                def rstd():
                    act.wait_ge(s_var, t + 1)
                    A(ln[:, :], pp[:, 1, :], ACT.Ln, bias=epsc[:, :]).then_inc(s_lv, 1)
                    act.wait_ge(s_lv, t + 1)
                    A(ln[:, :], ln[:, :], ACT.Exp, scale=-0.5).then_inc(s_rs, 1)

                def exp_of(v, limited, exp):
                    act.wait_ge(limited, t + 1)
                    A(v, v, ACT.Exp, scale=-1.0).then_inc(exp, 1)

                def log_of(v, exp, log):
                    act.wait_ge(exp, t + 1)
                    A(v, v, ACT.Ln, bias=1.0).then_inc(log, 1)

                def sigmoid_of(v, log, done):
                    act.wait_ge(log, t + 1)
                    A(v, v, ACT.Exp, scale=-1.0).then_inc(done, 1)

                def copy_z(par, h):
                    act.wait_ge(s_z, t * 2 + (h + 1))
                    if not start:
                        act.wait_ge(s_gate, t - 1)
                    A(sz[par][:, h, :], qp, ACT.Copy).then_inc(s_zc, 1)

                def copy_conv(par, h):
                    act.wait_ge(s_cv, t * 2 + (h + 1))
                    if not start and h == 0:
                        act.wait_ge(s_yv, t - 1)
                    A(u[par][:, h, :], pp[:, h, :], ACT.Identity, bias=cb[:, h:h + 1]).then_inc(s_cc, 1)

                def sigmoid_z(step):
                    if step == 0:
                        exp_of(exz, s_kz, s_ez)
                    if step == 1:
                        log_of(exz, s_ez, s_lz)
                    if step == 2:
                        sigmoid_of(exz, s_lz, s_rz)

                def sigmoid_c(step):
                    if step == 0:
                        exp_of(ex[:, :, :], s_kc, s_ec)
                    if step == 1:
                        log_of(ex[:, :, :], s_ec, s_lc)
                    if step == 2:
                        sigmoid_of(ex[:, :, :], s_lc, s_rc)

                def parts(par):
                    act.wait_ge(s_xd, t + 1)
                    A(bc[par][:, :], pp[0:96, 0, :], ACT.Copy).then_inc(s_hi, 1)
                    act.wait_ge(s_dt, t)
                    A(dts[96:104, :], pp[96:104, 0, :], ACT.Copy).then_inc(s_dts, 1)

                def middle(par):
                    act.wait_ge(s_rest, t + 1)
                    if not start:
                        act.wait_ge(s_o, t - 1)
                    A(bc[par][32:64, :], ln[32:64, :], ACT.Copy).then_inc(s_mid, 1)
                    A(mid, ln[64:96, :], ACT.Copy).then_inc(s_mid, 1)

                def absolute():
                    act.wait_ge(s_dt, t + 1)
                    act.wait_ge(s_u, t + 1)
                    for h in range(2):
                        m = A(ex[:, h, :], pp[:, h, :], ACT.Abs, bias=bdt[:, h:h + 1])
                    m.then_inc(s_ab, 1)

                def linear(par):
                    if not start:
                        act.wait_ge(s_du, t - 1)
                    for h in range(2):
                        m = A(delta[par][:, h, :], pp[:, h, :], ACT.Relu, bias=bdt[:, h:h + 1])
                    m.then_inc(s_rl, 1)

                def exp_abs():
                    act.wait_ge(s_ab, t + 1)
                    A(ex[:, :, :], ex[:, :, :], ACT.Exp, scale=-1.0).then_inc(s_ed, 1)

                def log_part():
                    act.wait_ge(s_ed, t + 1)
                    A(ex[:, :, :], ex[:, :, :], ACT.Ln, bias=1.0).then_inc(s_sp, 1)

                return square, rstd, copy_conv, sigmoid_c, copy_z, sigmoid_z, parts, middle, absolute, linear, exp_abs, log_part

            def decay(t, n, par):
                if n == 0:
                    act.wait_ge(s_del, t + 1)
                for h in range(2):
                    act.wait_ge(s_scan[h], t * NS + (n - 1))
                    A(dA[n % 2][:, h, :], delta[par][:, h, :], ACT.Exp, scale=a_neg[:, h, n:n + 1]).then_inc(s_dA[h], 1)

            def copy_c(t, n):
                act.wait_ge(s_C, t * NS + (n + 1))
                act.wait_ge(s_ch, t * NS + (n + 1 - CR))
                A(csb[n % CR], C_ps, ACT.Copy).then_inc(s_Ccp, 1)

            def layer0(t, pair, i, col, par, first, ahead):
                sq_, rs_, cc_, ec_, zc_, _, parts_, mi_, ab_, li_, ea_, lg_ = prep(t + 1)
                next_sq, next_rs = prep(t + 2)[:2]
                ez_ = prep(t)[5]
                for n in range(NS):
                    if n + 1 < NS:
                        decay(t, n + 1, par)
                    elif ahead:
                        decay(t + 1, 0, 1 - par)
                    if n in (3, 4, 5):
                        ez_(n - 3)
                    if ahead:
                        if n in (3, 5):
                            cc_(1 - par, (n - 3) // 2)
                        if n in (6, 7):
                            ec_(n - 6)
                        if n == 7:
                            ec_(2)
                        if n in (10, 13):
                            zc_(1 - par, (n - 10) // 3)
                        if n == 9:
                            parts_(1 - par)
                        if n == 10:
                            mi_(1 - par)
                        if n == 11:
                            ab_()
                        if n == 12:
                            ea_()
                            li_(1 - par)
                        if n == 13:
                            lg_()
                    if ahead == 2:
                        if n == NS - 2:
                            next_sq()
                        if n == NS - 1:
                            next_rs()
                    if n + 1 < NS:
                        copy_c(t, n + 1)
                    elif ahead:
                        copy_c(t + 1, 0)

            def features(t, par):
                def first_layer():
                    act.wait_ge(s_f1, t + 1)
                    act.wait_ge(s_f2, t)
                    A(f1, f_ps[0:64], ACT.Identity, bias=b1r[:, :]).then_inc(s_f1a, 1)

                def second_layer():
                    act.wait_ge(s_f2, t + 1)
                    act.wait_ge(s_gp, t)
                    A(f2, f_ps[0:32], ACT.Identity, bias=bs2[:, :]).then_inc(s_f2a, 1)

                def third_layer():
                    act.wait_ge(s_gp, t + 1)
                    A(g[par], f_ps, ACT.Copy).then_inc(s_g, 1)

                return first_layer, second_layer, third_layer

            def bias1(t, k, par):
                if k == 0:
                    act.wait_ge(s_g, t + 1)
                act.wait_ge(s_m2, t * (2 * NG) + 2 * (k - 3))
                for q in range(GQ - 2):
                    m = A(t1[k % 4][:, q, :], g[par], ACT.Identity, bias=ptb[:, GQ * k + q:GQ * k + q + 1])
                m.then_inc(s_t1, 1)

            def bias2(t, k, half):
                act.wait_ge(s_m2, t * (2 * NG) + (2 * k + half + 1))
                if half == 0:
                    act.wait_ge(s_m3, t * NG + (k - 3))
                A(t2[k % 4][:, 2 * half:2 * half + 2, :], m2_ps[half], ACT.Identity, bias=bm2[:, :]).then_inc(s_t2, 1)

            def bias3(t, k):
                act.wait_ge(s_m3, t * NG + (k + 1))
                act.wait_ge(s_m4, t * (NG // 2) + (k // 2 - 1))
                act.wait_ge(s_l3, t * NG + (k - 1))
                A(t3[k % 4], m3_ps, ACT.Relu, bias=bm3s[:, 1:2], scale=1 - SLOPE)
                A(t3s[k % 2], m3_ps, ACT.Identity, bias=bm3s[:, 0:1], scale=SLOPE).then_inc(s_t3, 1)

            def sdf(t):
                act.wait_ge(s_lim, t + 1)
                A(sg, sg, ACT.Exp, scale=-1.0).then_inc(s_e, 1)
                act.wait_ge(s_e, t + 1)
                A(sg, sg, ACT.Ln, bias=1.0).then_inc(s_le, 1)
                act.wait_ge(s_le, t + 1)
                A(sg, sg, ACT.Exp, scale=-1.0).then_inc(s_sg, 1)

            def layer1(t, pair, i, col, par, first, ahead):
                f_a, f_b, f_c = features(t + 1, 1 - par)
                for k in range(NG):
                    bias2(t, k, 0)
                    nxt = (t, k + 2, par) if k + 2 < NG else (t + 1, k + 2 - NG, 1 - par)
                    if k + 2 < NG or ahead:
                        bias1(*nxt)
                    bias2(t, k, 1)
                    if k >= 2:
                        bias3(t, k - 2)
                    elif not first:
                        bias3(t - 1, NG - 2 + k)
                    if k == 5 and not first:
                        sdf(t - 1)
                    if ahead:
                        if k == 0:
                            f_a()
                        if k == 2:
                            f_b()
                        if k == 4:
                            f_c()

            act.wait_ge(s_dve0, 1)
            with act.Fori(0, B) as b:
                t0 = fresh(act, b * T + 1)
                group_norm(b * 2)
                act.wait_ge(s_nb, b * 2 + 1)
                sq_, rs_, cc_, ec_, zc_, ez_, parts_, mi_, ab_, li_, ea_, lg_ = prep(t0, True)
                sq_()
                rs_()
                for h in range(2):
                    cc_(0, h)
                for step in range(3):
                    ec_(step)
                for h in range(2):
                    zc_(0, h)
                parts_(0)
                mi_(0)
                ab_()
                li_(0)
                ea_()
                lg_()
                decay(t0, 0, 0)
                copy_c(t0, 0)
                for f in prep(t0 + 1)[:2]:
                    f()
                walk(act, b, layer0)
                group_norm(b * 2 + 1)
                act.wait_ge(s_nb, b * 2 + 2)
                t1st = fresh(act, b * T + 1)
                for f in features(t1st, 0):
                    f()
                for k in range(2):
                    bias1(t1st, k, 0)
                walk(act, b, layer1)
                t9 = fresh(act, b * T + T)
                bias3(t9, NG - 2)
                bias3(t9, NG - 1)
                sdf(t9)

        @block.gpsimd
        def _(pool):
            chunk_zero(pool, pool_counts)

            def gate(t, par):
                pool.wait_ge(s_yv, t + 1)
                pool.wait_ge(s_sz, t + 1)
                nc.gpsimd.tensor_tensor(yo, yo, sz[par], ALU.mult).then_inc(s_gate, 1)

            def times_c(t, n):
                pool.wait_ge(s_Ccp, t * NS + (n + 1))
                pool.wait_ge(s_scan[0], t * NS + (n + 1))
                pool.wait_ge(s_scan[1], t * NS + (n + 1))
                pool.wait_ge(s_sum, t * NS + (n + 1 - CR))
                c = csb[n % CR].rearrange("p (o l) -> p o l", o=1).to_broadcast([P, 2, L])
                nc.gpsimd.tensor_tensor(ch[n % CR], H[:, n % HR, :, :], c, ALU.mult).then_inc(s_ch, 1)

            def add_pair(t, n):
                pool.wait_ge(s_ch, t * NS + (n + 1))
                nc.gpsimd.tensor_tensor(ch[n % CR], ch[n % CR], ch[(n - 1) % CR], ALU.add).then_inc(s_pair, 1)

            def silu_c(t, par):
                pool.wait_ge(s_rc, t + 1)
                nc.gpsimd.tensor_tensor(u[par], u[par], ex[:, :, :], ALU.mult).then_inc(s_u, 1)

            def silu_z(t, par):
                pool.wait_ge(s_rz, t + 1)
                nc.gpsimd.tensor_tensor(sz[par], sz[par], exz, ALU.mult).then_inc(s_sz, 1)

            def layer0(t, pair, i, col, par, first, ahead):
                for n in range(NS):
                    if n == 8 and ahead:
                        silu_c(t + 1, 1 - par)
                    times_c(t, n)
                    if n in PAIRED:
                        add_pair(t, n)
                    if n == 14:
                        silu_z(t, par)
                    if n == 3 and not first:
                        gate(t - 1, 1 - par)

            def bias1_last(t, k, par):
                if k == 0:
                    pool.wait_ge(s_g, t + 1)
                pool.wait_ge(s_m2, t * (2 * NG) + 2 * (k - 3))
                q = GQ * k + GQ - 2
                features = g[par].rearrange("p (o l) -> p o l", o=1).to_broadcast([P, 2, L])
                quads = ptb[:, q:q + 2].rearrange("p (q o) -> p q o", o=1).to_broadcast([P, 2, L])
                nc.gpsimd.tensor_tensor(t1[k % 4][:, GQ - 2:, :], features, quads, ALU.add).then_inc(s_t1p, 1)

            def leaky3(t, k):
                pool.wait_ge(s_t3, t * NG + (k + 1))
                nc.gpsimd.tensor_tensor(t3[k % 4], t3[k % 4], t3s[k % 2], ALU.add).then_inc(s_l3, 1)

            def layer1(t, pair, i, col, par, first, ahead):
                for k in range(NG):
                    if k + 2 < NG:
                        bias1_last(t, k + 2, par)
                    elif ahead:
                        bias1_last(t + 1, k + 2 - NG, 1 - par)
                    if k >= 2:
                        leaky3(t, k - 2)
                    elif not first:
                        leaky3(t - 1, NG - 2 + k)

            with pool.Fori(0, B) as b:
                t0 = fresh(pool, b * T + 1)
                silu_c(t0, 0)
                walk(pool, b, layer0)
                gate(b * T + T, 1)
                t1st = fresh(pool, b * T + 1)
                bias1_last(t1st, 0, 0)
                bias1_last(t1st, 1, 0)
                walk(pool, b, layer1)
                t9 = fresh(pool, b * T + T)
                leaky3(t9, NG - 2)
                leaky3(t9, NG - 1)

        @block.vector
        def _(dve):
            V = nc.vector
            chunk_zero(dve, dve_counts)
            for k in range(4):
                dve.wait_ge(s_x0[k], 16)
                with dve.Fori(0, T // 4) as i:
                    st = stats[:, bass.ds(i + k * (T // 4), 1), :].rearrange("p o s -> p (o s)")
                    V.bn_stats(st, X[:, bass.ds(i * L + k * (N // 4), L)]).then_inc(s_st, 1)
            dve.wait_ge(s_w, W_ALL)
            V.memset(epsc[:, :], EPS).then_inc(s_dve0, 1)
            win = w_x.rearrange("p (o n) -> p o n", o=1).to_broadcast([P, TAPS, 2 * P])
            V.tensor_tensor(w_conv[:, :, :, :].rearrange("p k h n -> p k (h n)"), tapw, win, ALU.mult).then_inc(s_dve0, 1)
            dve.wait_ge(s_act0, 1)
            V.tensor_scalar(a_neg[:, :, :], a_neg[:, :, :], -1.0, None, ALU.mult).then_inc(s_dve0, 1)
            dve.wait_ge(s_pe0, 2)
            V.tensor_copy(gw[:, :], ps[0:32, 0, 0:P]).then_inc(s_dve0, 1)
            V.tensor_tensor(gb[:, :], bm1[:, :], ps[:, 1, 0:1], ALU.add).then_inc(s_dve0, 1)
            V.tensor_scalar(bm3s[:, 0:1], bm3[:, :], SLOPE, None, ALU.mult).then_inc(s_dve0, 1)
            V.tensor_scalar(bm3s[:, 1:2], bm3[:, :], 1 - SLOPE, None, ALU.mult).then_inc(s_dve0, 1)
            dve.wait_ge(s_dve0, 7)
            V.tensor_scalar(ptb[:, :], pts[:, :], m1p[:, :], gb[:, :], ALU.mult, ALU.add).then_inc(s_dve0, 1)
            dve.wait_ge(s_dve0, 8)

            def group_norm(k):
                plain(dve)
                V.bn_aggr(mv[:, :], stats[:, :, :]).then_inc(s_mv, 1)
                dve.wait_ge(s_gm, k + 1)
                dve.wait_ge(s_mv, k + 1)
                V.tensor_tensor(dev[:, :], mv[:, 0:1], pp[:, 0, 0:1], ALU.subtract).then_inc(s_dev, 1)
                dve.wait_ge(s_dev, k + 1)
                V.scalar_tensor_tensor(out=vd[:, :], in0=dev[:, :], scalar=dev[:, :], in1=mv[:, 1:2],
                                       op0=ALU.mult, op1=ALU.add).then_inc(s_vd, 1)
                dve.wait_ge(s_gr, k + 1)
                V.scalar_tensor_tensor(out=gs[:, :], in0=pp[:, 0, 0:1], scalar=-1.0, in1=gr[:, :],
                                       op0=ALU.mult, op1=ALU.mult).then_inc(s_gs, 1)
                dve.wait_ge(s_cs, k + 1)

            def prep(t):
                def normed():
                    dve.wait_ge(s_rs, t + 1)
                    V.scalar_tensor_tensor(out=ln[:, :], in0=pp[:, 0, :], scalar=cs[:, :], in1=ln[:, :],
                                           op0=ALU.add, op1=ALU.mult).then_inc(s_xn, 1)

                def affine(carry):
                    dve.wait_ge(s_cv, t * 2)
                    dve.wait_ge(s_z, t * 2)
                    if carry:
                        V.tensor_copy(xnf[:, 0:TAPS - 1], xnf[:, L:L + TAPS - 1]).then_inc(s_car, 1)
                    else:
                        V.memset(xnf[:, 0:TAPS - 1], 0.0).then_inc(s_car, 1)
                    dve.wait_ge(s_car, t + 1)
                    dve.wait_ge(s_xn, t + 1)
                    V.tensor_scalar(xnf[:, TAPS - 1:], ln[:, :], lnw[:, :], lnb[:, :], ALU.mult, ALU.add).then_inc(s_xnf, 1)

                def limit_c(par):
                    dve.wait_ge(s_cc, t * 2 + 2)
                    V.tensor_scalar(ex[:, :, :], u[par], SIGMOID_ZERO, None, ALU.max).then_inc(s_kc, 1)

                def limit_z(par):
                    dve.wait_ge(s_zc, t * 2 + 2)
                    dve.wait_ge(s_sz, t)
                    V.tensor_scalar(exz, sz[par], SIGMOID_ZERO, None, ALU.max).then_inc(s_kz, 1)

                def parts(par):
                    dve.wait_ge(s_hi, t + 1)
                    dve.wait_ge(s_xnf, t + 1)
                    V.tensor_tensor(ln[0:96, :], pp[0:96, 0, :], bc[par][:, :], ALU.subtract).then_inc(s_rest, 1)

                def low_part(par):
                    dve.wait_ge(s_mid, t * 2 + 2)
                    V.tensor_tensor(bc[par][64:96, :], ln[64:96, :], mid, ALU.subtract).then_inc(s_lo, 1)

                def step_size(par):
                    dve.wait_ge(s_sp, t + 1)
                    dve.wait_ge(s_rl, t + 1)
                    V.tensor_tensor(delta[par], delta[par], ex[:, :, :], ALU.add).then_inc(s_del, 1)

                def step_u(par):
                    dve.wait_ge(s_del, t + 1)
                    dve.wait_ge(s_mulb, t * NS)
                    V.tensor_tensor(du, delta[par], u[par], ALU.mult).then_inc(s_du, 1)

                return normed, affine, limit_c, limit_z, parts, low_part, step_size, step_u

            def times_b(t, n, par):
                dve.wait_ge(s_B, t * NS + (n + 1))
                dve.wait_ge(s_scan[1], t * NS + (n - 3))
                if n == 0:
                    dve.wait_ge(s_du, t + 1)
                bb = B_ps[n % 2].rearrange("p (o l) -> p o l", o=1).to_broadcast([P, 2, L])
                V.tensor_tensor(dbu[n % 4], du, bb, ALU.mult).then_inc(s_mulb, 1)

            def keep_last(t, n, first):
                if n == 0 and first:
                    dve.sem_inc(s_last, 1)
                    return
                dve.wait_ge(s_scan[0], t * NS + n)
                dve.wait_ge(s_scan[1], t * NS + n)
                m, k = (n - 4) % NS, (n - 4) % HR
                V.tensor_copy(carried[:, m:m + 4, :], H[:, k:k + 4, :, L - 1]).then_inc(s_last, 1)

            def scan(t, n):
                dve.wait_ge(s_mulb, t * NS + (n + 1))
                dve.wait_ge(s_ch, t * NS + (n + 1 - HR))
                dve.wait_ge(s_last, t * (NS // 4) + n // 4)
                for h in range(2):
                    dve.wait_ge(s_dA[h], t * NS + (n + 1))
                    V.tensor_tensor_scan(H[:, n % HR, h, :], dA[n % 2][:, h, :], dbu[n % 4][:, h, :],
                                         carried[:, n, h:h + 1], ALU.mult, ALU.add).then_inc(s_scan[h], 1)

            def y_out(t, par):
                dve.wait_ge(s_sum, t * NS + NS)
                dve.wait_ge(s_o, t)
                for h in range(2):
                    m = V.scalar_tensor_tensor(out=yo[:, h, :], in0=u[par][:, h, :], scalar=dsk[:, h:h + 1],
                                               in1=y_ps[:, h, :], op0=ALU.mult, op1=ALU.add)
                m.then_inc(s_yv, 1)

            def residual(t, col):
                xc = X[:, bass.ds(col, L)]
                dve.wait_ge(s_o, t + 1)
                V.tensor_tensor(xc, xc, qp, ALU.add).then_inc(s_res, 1)

            def residual_stats(t, col, i):
                st = stats[:, bass.ds(i, 1), :].rearrange("p o s -> p (o s)")
                dve.wait_ge(s_res, t + 1)
                plain(dve)
                V.bn_stats(st, X[:, bass.ds(col, L)]).then_inc(s_st1, 1)

            def layer0(t, pair, i, col, par, first, ahead):
                n_, a_, lc_, _, pa_, lo_, de_, du_ = prep(t + 1)
                lz_ = prep(t)[3]
                for n in range(NS):
                    if n + 1 < NS:
                        times_b(t, n + 1, par)
                    elif ahead:
                        times_b(t + 1, 0, 1 - par)
                    if n % 4 == 0:
                        keep_last(t, n, first)
                    scan(t, n)
                    if n == 2 and not first:
                        y_out(t - 1, 1 - par)
                    if n == 8 and not first:
                        residual(t - 1, col - L)
                    if n == 9 and not first:
                        residual_stats(t - 1, col - L, i - 1)
                    if n == 1:
                        lz_(par)
                    if ahead:
                        if n == 0:
                            n_()
                            a_(True)
                        if n == 6:
                            lc_(1 - par)
                        if n == 10:
                            pa_(1 - par)
                        if n == 11:
                            lo_(1 - par)
                        if n == 14:
                            de_(1 - par)
                            du_(1 - par)

            def leaky(ap, s):
                V.scalar_tensor_tensor(out=ap, in0=ap, scalar=SLOPE, in1=ap, op0=ALU.mult, op1=ALU.max).then_inc(s, 1)

            def features(t):
                def first_layer():
                    dve.wait_ge(s_f1a, t + 1)
                    leaky(f1, s_f1l)

                def second_layer():
                    dve.wait_ge(s_f2a, t + 1)
                    leaky(f2, s_f2l)

                return first_layer, second_layer

            def flat(ap):
                return ap.rearrange("p k l -> p (k l)")

            def leaky1(t, k):
                dve.wait_ge(s_t1, t * NG + (k + 1))
                dve.wait_ge(s_t1p, t * NG + (k + 1))
                leaky(flat(t1[k % 4]), s_l1)

            def leaky2(t, k):
                dve.wait_ge(s_t2, t * (2 * NG) + (2 * k + 2))
                leaky(flat(t2[k % 4]), s_l2)

            def limit(t):
                dve.wait_ge(s_m4, t * (NG // 2) + NG // 2)
                dve.wait_ge(s_ob, t)
                V.tensor_scalar(sg, m4_ps, bm4[:, :], SIGMOID_ZERO, ALU.add, ALU.max).then_inc(s_lim, 1)

            def sdf(t, col, par):
                dve.wait_ge(s_sg, t + 1)
                V.tensor_tensor(ob[par], sg, X[:, bass.ds(col, L)], ALU.add).then_inc(s_ob, 1)

            def layer1(t, pair, i, col, par, first, ahead):
                f_a, f_b = features(t + 1)
                second = isinstance(i, int) and i == 1
                for k in range(NG):
                    if k + 1 < NG:
                        leaky1(t, k + 1)
                    elif ahead:
                        leaky1(t + 1, 0)
                    leaky2(t, k)
                    if k == 4 and not first:
                        limit(t - 1)
                    if k == 6 and not first:
                        if par == 1:
                            dve.wait_ge(s_out[0], pair * 16)
                        else:
                            dve.wait_ge(s_out[1], (pair - 1) * 16)
                        sdf(t - 1, col - L, 1 - par)
                    if k == 7 and not (first or second):
                        next_stats(pair - 1, col - 2 * L, i - 2, par)
                    if ahead:
                        if k == 1:
                            f_a()
                        if k == 3:
                            f_b()

            def next_stats(pair, col, i, par):
                dve.wait_ge(s_x[par], pair * 16)
                plain(dve)
                st = stats[:, bass.ds(i, 1), :].rearrange("p o s -> p (o s)")
                V.bn_stats(st, X[:, bass.ds(col, L)]).then_inc(s_st, 1)

            with dve.Fori(0, B) as b:
                t0 = fresh(dve, b * T + 1)
                for par in range(2):
                    dve.wait_ge(s_out[par], b * (16 * PAIRS) + 16)
                dve.wait_ge(s_st, (b + 1) * T)
                group_norm(b * 2)
                V.tensor_scalar(cen_r[:, :], cen[:, :], gr[:, :], None, ALU.mult).then_inc(s_agg, 1)
                V.tensor_copy(cs[:, :], ps[:, 7, 0:1]).then_inc(s_h0, 1)
                V.memset(carried[:, :, :], 0.0).then_inc(s_h0, 1)
                dve.wait_ge(s_agg, b * 2 + 1)
                dve.wait_ge(s_h0, (b + 1) * 2)
                dve.sem_inc(s_nb, 1)
                n_, a_, lc_, lz_, pa_, lo_, de_, du_ = prep(t0)
                n_()
                a_(False)
                lc_(0)
                pa_(0)
                lo_(0)
                de_(0)
                du_(0)
                times_b(t0, 0, 0)

                walk(dve, b, layer0)
                t9 = fresh(dve, b * T + T)
                y_out(t9, 1)
                residual(t9, (T - 1) * L)
                residual_stats(t9, (T - 1) * L, T - 1)
                dve.wait_ge(s_st1, t9 + 1)

                group_norm(b * 2 + 1)
                V.tensor_scalar(s1r[:, :], s1[:, :], gr[:, :], None, ALU.mult).then_inc(s_agg, 1)
                V.tensor_tensor(b1r[:, :], bs1[:, :], ps[0:64, 7, 0:1], ALU.add).then_inc(s_nw, 1)
                dve.wait_ge(s_agg, b * 2 + 2)
                dve.wait_ge(s_nw, b + 1)
                dve.sem_inc(s_nb, 1)
                t1st = fresh(dve, b * T + 1)
                for f in features(t1st):
                    f()
                leaky1(t1st, 0)
                walk(dve, b, layer1)
                t9 = fresh(dve, b * T + T)
                limit(t9)
                dve.wait_ge(s_out[1], (b * PAIRS + PAIRS) * 16)
                sdf(t9, (T - 1) * L, 1)
                for par in range(2):
                    next_stats(fresh(dve, b * PAIRS + PAIRS), N - (2 - par) * L, T - 2 + par, par)


def kernel(**inputs):
    import numpy as np
    import concourse.bacc as bacc
    import ml_dtypes
    from concourse import mybir as mb
    from concourse.bass_utils import run_bass_kernel_spmd as run

    q = {k: np.ascontiguousarray(v) for k, v in inputs.items()}
    B, C, Hh, Ww = q["x"].shape
    f = np.float32

    def halves(a):
        return np.ascontiguousarray(a.reshape(2, P, -1).transpose(1, 0, 2))

    def col(a):
        return np.ascontiguousarray(a.reshape(-1, 1))

    xp_t = q["L0_conv_W_xproj"].T
    xp_t = np.concatenate([xp_t[:, DTR:]] * 3 + [xp_t[:, :DTR]], axis=1)
    mw1, mw2, mw3, mw4 = (q[f"L1_conv_mw{i}"] for i in (1, 2, 3, 4))
    mw2_bd = np.zeros((P, P), f)
    mw3_bd = np.zeros((P, 64), f)
    mw4_bd = np.zeros((P, 4, 32), f)
    for j in range(4):
        mw2_bd[32 * j:32 * j + 32, 32 * j:32 * j + 32] = mw2.T
        mw3_bd[32 * j:32 * j + 32, 16 * j:16 * j + 16] = mw3.T
    for k in range(4):
        for j in range(8):
            mw4_bd[16 * j:16 * j + 16, k, 8 * k + j] = mw4[0]
    eye = np.eye(P, dtype=f)
    c = np.arange(P)
    gm = ((c[:, None] // 4) == (c[None, :] // 4)).astype(f) / 4
    om = np.full((P, 1), 1.0 / P, f)
    pick = np.zeros((96, 2 * NS), ml_dtypes.bfloat16)
    for k in range(96):
        pick[k, k % 32] = 1
    lin = np.linspace(-1.0, 1.0, P, dtype=f)
    points = np.zeros((P, NG * GQ), f)
    for quad in range(NG * GQ):
        s, e = quad // 2, quad % 2
        for j in range(4):
            points[32 * j:32 * j + 32, quad] = lin[32 * (s % 4) + 8 * (s // 4) + 4 * e + j]

    arrays = dict(
        x=q["x"].reshape(B, C, Hh * Ww),
        w_in_t=np.ascontiguousarray(q["L0_conv_W_in"].T),
        conv_w_t=np.ascontiguousarray(q["L0_conv_conv_w"].T),
        conv_b=halves(q["L0_conv_conv_b"].reshape(-1, 1))[:, :, 0],
        ln_w=col(q["L0_conv_ln_w"]), ln_b=col(q["L0_conv_ln_b"]),
        w_xproj_t=halves(xp_t),
        w_dt_t=np.ascontiguousarray(q["L0_conv_W_dt"].T.reshape(DTR, 2, P)),
        b_dt=halves(q["L0_conv_b_dt"].reshape(-1, 1))[:, :, 0],
        a_log=halves(q["L0_conv_A_log"]),
        d_skip=halves(q["L0_conv_D"].reshape(-1, 1))[:, :, 0],
        w_out_t=halves(q["L0_conv_W_out"].T),
        sw1_t=q["L1_conv_sw1"].T, sb1=col(q["L1_conv_sb1"]), sw2_t=q["L1_conv_sw2"].T, sb2=col(q["L1_conv_sb2"]),
        sw3=q["L1_conv_sw3"], sb3=col(q["L1_conv_sb3"]),
        mw1_t=np.tile(mw1[:, :16].T, (1, 4)), mw1_pt=col(np.tile(mw1[:, 16], 4)), mb1=col(np.tile(q["L1_conv_mb1"], 4)),
        mw2_bd=mw2_bd, mb2=col(np.tile(q["L1_conv_mb2"], 4)), mw3_bd=mw3_bd, mb3=col(np.tile(q["L1_conv_mb3"], 8)),
        mw4_bd=mw4_bd, mb4=col(np.tile(q["L1_conv_mb4"], P)),
        center=eye - 1.0 / f(P), group_mean=gm, ones_mean=om, ident=eye, pick=pick, points=points,
    )
    nc = bacc.Bacc("TRN2", target_bir_lowering=False, num_devices=1)
    feed, args = {}, []
    for name, a in arrays.items():
        a = np.ascontiguousarray(a)
        feed["in_" + name] = a
        args.append(nc.dram_tensor("in_" + name, a.shape, mb.dt.from_np(a.dtype), kind="ExternalInput").ap())
    out = nc.dram_tensor("out", (B, C, Hh * Ww), mb.dt.float32, kind="ExternalOutput").ap()
    mamba_sdf_kernel(nc, *args, out)
    r = run(nc, [feed], core_ids=[0])
    return r.results[0]["out"].reshape(B, C, Hh, Ww)
```
